# Optimizing a Trainium2 kernel written in Bass

```python
import numpy as np
import jax
import jax.numpy as jnp

def _softmax(x, axis=-1):
    return jax.nn.softmax(x, axis=axis)

def _gelu(x):
    return jax.nn.gelu(x, approximate=True)

def _silu(x):
    return jax.nn.silu(x)

def _sigmoid(x):
    return jax.nn.sigmoid(x)

def _layernorm(x, axis=-1, eps=1e-05):
    m = jnp.mean(x, axis=axis, keepdims=True)
    v = jnp.var(x, axis=axis, keepdims=True)
    return (x - m) / jnp.sqrt(v + eps)

def _scatter_add(tgt, idx, src, axis=0):
    return tgt.at[idx].add(src)

def _segment_sum(src, seg, n):
    return jax.ops.segment_sum(src, seg, n)
kernel_name = 'mk_seq_preln_d1_jaxref_r8_145813'

def setup_inputs(seed: int=0):
    np.random.seed(seed)
    _w = jnp.asarray

    def _L0_attn_setup():
        import jax, jax.numpy as jnp
        import numpy as np
        import math
        B, S, DIM = (2, 256, 128)
        H, KVH = (16, 4)
        HD = DIM // H
        WINDOW = 32
        ROPE_BASE = 10000.0
        EPS = 1e-06

        def _rms_norm(v):
            return v * jax.lax.rsqrt(jnp.mean(v * v, axis=-1, keepdims=True) + EPS)

        def _rope_tables(seqlen, dtype):
            inv_freq = 1.0 / ROPE_BASE ** (jnp.arange(0, HD, 2, dtype=jnp.float32) / HD)
            t = jnp.arange(seqlen, dtype=jnp.float32)
            freqs = jnp.outer(t, inv_freq)
            return (jnp.cos(freqs).astype(dtype)[None, None], jnp.sin(freqs).astype(dtype)[None, None])

        def _apply_rotary(v, cos, sin):
            half = v.shape[-1] // 2
            v1, v2 = (v[..., :half], v[..., half:])
            return jnp.concatenate((v1 * cos + v2 * sin, -v1 * sin + v2 * cos), axis=-1)
        key = jax.random.key(seed)
        ks = jax.random.split(key, 6)
        s = 0.02
        return {'x': jax.random.normal(ks[0], (B, S, DIM), jnp.float32), 'Wq': jax.random.normal(ks[1], (DIM, DIM), jnp.float32) * s, 'Wk': jax.random.normal(ks[2], (KVH * HD, DIM), jnp.float32) * s, 'Wv': jax.random.normal(ks[3], (KVH * HD, DIM), jnp.float32) * s, 'Wo': jax.random.normal(ks[4], (DIM, DIM), jnp.float32) * s, 'q_gain': jnp.ones((H,), jnp.float32), 'pair_mix': jnp.tile(jnp.eye(2, dtype=jnp.float32), (H // 2, 1, 1)) + 0.01 * jax.random.normal(ks[5], (H // 2, 2, 2), jnp.float32)}
    _L0_attn_in = _L0_attn_setup()

    def _L0_ffn_setup():
        import jax, jax.numpy as jnp
        import numpy as np
        JITTER_EPS = 0.01
        NEG_INF = -jnp.inf

        def sparsemixer_eval(scores, jitter_eps):
            m1 = jnp.max(scores, axis=-1, keepdims=True)
            ind1 = jnp.argmax(scores, axis=-1)
            factor1 = jnp.maximum(jnp.abs(scores), m1)
            mask1 = jax.lax.stop_gradient((m1 - scores) / factor1 > 2.0 * jitter_eps)
            gates1 = jax.nn.softmax(jnp.where(mask1, NEG_INF, scores), axis=-1)
            mult1 = jnp.take_along_axis(gates1, ind1[:, None], axis=-1)[:, 0]
            E = scores.shape[-1]
            onehot1 = ind1[:, None] == jnp.arange(E)[None, :]
            masked_scores = jnp.where(onehot1, NEG_INF, scores)
            m2 = jnp.max(masked_scores, axis=-1, keepdims=True)
            ind2 = jnp.argmax(masked_scores, axis=-1)
            factor2 = jnp.maximum(jnp.abs(scores), m2)
            mask2 = jax.lax.stop_gradient((m2 - scores) / factor2 > 2.0 * jitter_eps)
            gates2 = jax.nn.softmax(jnp.where(mask2, NEG_INF, masked_scores), axis=-1)
            mult2 = jnp.take_along_axis(gates2, ind2[:, None], axis=-1)[:, 0]
            multiplier = jnp.stack([mult1, mult2], axis=-1)
            selected = jnp.stack([ind1, ind2], axis=-1)
            return (multiplier, selected)
        key = jax.random.key(seed)
        k0, k1, k2, k3, k4 = jax.random.split(key, 5)
        B, S, H, F, E = (2, 128, 128, 256, 8)
        scale = 0.02
        return {'hidden_states': jax.random.normal(k0, (B, S, H), dtype=jnp.float32), 'router_w': jax.random.normal(k1, (E, H), dtype=jnp.float32) * scale, 'w_gate': jax.random.normal(k2, (E, F, H), dtype=jnp.float32) * scale, 'w_up': jax.random.normal(k3, (E, F, H), dtype=jnp.float32) * scale, 'w_down': jax.random.normal(k4, (E, H, F), dtype=jnp.float32) * scale}
    _L0_ffn_in = _L0_ffn_setup()
    _d = {'L0_attn_x': _L0_attn_in['x'], 'L0_attn_Wq': _L0_attn_in['Wq'], 'L0_attn_Wk': _L0_attn_in['Wk'], 'L0_attn_Wv': _L0_attn_in['Wv'], 'L0_attn_Wo': _L0_attn_in['Wo'], 'L0_attn_q_gain': _L0_attn_in['q_gain'], 'L0_attn_pair_mix': _L0_attn_in['pair_mix'], 'L0_ffn_router_w': _L0_ffn_in['router_w'], 'L0_ffn_w_gate': _L0_ffn_in['w_gate'], 'L0_ffn_w_up': _L0_ffn_in['w_up'], 'L0_ffn_w_down': _L0_ffn_in['w_down']}
    _x0 = _d['L0_attn_x']
    _d['L0_attn_x'] = jax.random.normal(jax.random.fold_in(jax.random.key(seed), 1), (16, 512, 128), dtype=_x0.dtype)
    del _x0
    return _d

def reference(L0_attn_x, L0_attn_Wq, L0_attn_Wk, L0_attn_Wv, L0_attn_Wo, L0_attn_q_gain, L0_attn_pair_mix, L0_ffn_router_w, L0_ffn_w_gate, L0_ffn_w_up, L0_ffn_w_down):

    def _L0_attn_ref(x, Wq, Wk, Wv, Wo, q_gain, pair_mix):
        import jax, jax.numpy as jnp
        import numpy as np
        import math
        B, S, DIM = (2, 256, 128)
        H, KVH = (16, 4)
        HD = DIM // H
        WINDOW = 32
        ROPE_BASE = 10000.0
        EPS = 1e-06

        def _rms_norm(v):
            return v * jax.lax.rsqrt(jnp.mean(v * v, axis=-1, keepdims=True) + EPS)

        def _rope_tables(seqlen, dtype):
            inv_freq = 1.0 / ROPE_BASE ** (jnp.arange(0, HD, 2, dtype=jnp.float32) / HD)
            t = jnp.arange(seqlen, dtype=jnp.float32)
            freqs = jnp.outer(t, inv_freq)
            return (jnp.cos(freqs).astype(dtype)[None, None], jnp.sin(freqs).astype(dtype)[None, None])

        def _apply_rotary(v, cos, sin):
            half = v.shape[-1] // 2
            v1, v2 = (v[..., :half], v[..., half:])
            return jnp.concatenate((v1 * cos + v2 * sin, -v1 * sin + v2 * cos), axis=-1)
        bsz, seqlen, dim = x.shape
        q = (x @ Wq.T).reshape(bsz, seqlen, H, HD).transpose(0, 2, 1, 3)
        k = (x @ Wk.T).reshape(bsz, seqlen, KVH, HD).transpose(0, 2, 1, 3)
        v = (x @ Wv.T).reshape(bsz, seqlen, KVH, HD).transpose(0, 2, 1, 3)
        q = _rms_norm(q)
        k = _rms_norm(k)
        cos, sin = _rope_tables(seqlen, q.dtype)
        q = _apply_rotary(q, cos, sin)
        k = _apply_rotary(k, cos, sin)
        q = q * q_gain.astype(q.dtype)[None, :, None, None]
        rep = H // KVH
        k_full = jnp.repeat(k, rep, axis=1)
        v_full = jnp.repeat(v, rep, axis=1)
        pos = jnp.arange(seqlen)
        mask = (pos[:, None] >= pos[None, :]) & (pos[:, None] - pos[None, :] < WINDOW)
        scale = 1.0 / math.sqrt(HD)
        scores = jnp.einsum('bhqd,bhkd->bhqk', q, k_full) * scale
        scores = jnp.where(mask[None, None], scores, jnp.finfo(scores.dtype).min)
        att = jax.nn.softmax(scores, axis=-1)
        y = jnp.einsum('bhqk,bhkd->bhqd', att, v_full)
        yp = y.reshape(bsz, H // 2, 2, seqlen, HD)
        y = jnp.einsum('bpitd,poi->bpotd', yp, pair_mix.astype(y.dtype)).reshape(bsz, H, seqlen, HD)
        out = y.transpose(0, 2, 1, 3).reshape(bsz, seqlen, dim) @ Wo.T
        return out

    def _L0_ffn_ref(hidden_states, router_w, w_gate, w_up, w_down):
        import jax, jax.numpy as jnp
        import numpy as np
        JITTER_EPS = 0.01
        NEG_INF = -jnp.inf

        def sparsemixer_eval(scores, jitter_eps):
            m1 = jnp.max(scores, axis=-1, keepdims=True)
            ind1 = jnp.argmax(scores, axis=-1)
            factor1 = jnp.maximum(jnp.abs(scores), m1)
            mask1 = jax.lax.stop_gradient((m1 - scores) / factor1 > 2.0 * jitter_eps)
            gates1 = jax.nn.softmax(jnp.where(mask1, NEG_INF, scores), axis=-1)
            mult1 = jnp.take_along_axis(gates1, ind1[:, None], axis=-1)[:, 0]
            E = scores.shape[-1]
            onehot1 = ind1[:, None] == jnp.arange(E)[None, :]
            masked_scores = jnp.where(onehot1, NEG_INF, scores)
            m2 = jnp.max(masked_scores, axis=-1, keepdims=True)
            ind2 = jnp.argmax(masked_scores, axis=-1)
            factor2 = jnp.maximum(jnp.abs(scores), m2)
            mask2 = jax.lax.stop_gradient((m2 - scores) / factor2 > 2.0 * jitter_eps)
            gates2 = jax.nn.softmax(jnp.where(mask2, NEG_INF, masked_scores), axis=-1)
            mult2 = jnp.take_along_axis(gates2, ind2[:, None], axis=-1)[:, 0]
            multiplier = jnp.stack([mult1, mult2], axis=-1)
            selected = jnp.stack([ind1, ind2], axis=-1)
            return (multiplier, selected)
        B, S, H = hidden_states.shape
        E = router_w.shape[0]
        x = hidden_states.reshape(-1, H)
        T = x.shape[0]
        logits = x @ router_w.T
        routing_weights, selected = sparsemixer_eval(logits, JITTER_EPS)
        tok = jnp.arange(T)
        dense_w = jnp.zeros((T, E), dtype=x.dtype)
        dense_w = dense_w.at[tok, selected[:, 0]].add(routing_weights[:, 0])
        dense_w = dense_w.at[tok, selected[:, 1]].add(routing_weights[:, 1])
        out = jnp.zeros_like(x)
        for e in range(E):
            h = jax.nn.silu(x @ w_gate[e].T) * (x @ w_up[e].T)
            out = out + dense_w[:, e:e + 1] * (h @ w_down[e].T)
        return out.reshape(B, S, H)
    x = L0_attn_x
    x = x + _L0_attn_ref(_layernorm(x, axis=-1), L0_attn_Wq, L0_attn_Wk, L0_attn_Wv, L0_attn_Wo, L0_attn_q_gain, L0_attn_pair_mix)
    x = x + _L0_ffn_ref(_layernorm(x, axis=-1), L0_ffn_router_w, L0_ffn_w_gate, L0_ffn_w_up, L0_ffn_w_down)
    return x

_drawn_inputs = setup_inputs


def setup_inputs(seed=0):
    import zlib

    import numpy as np

    out = dict(_drawn_inputs(seed))
    spreads = {'L0_attn_q_gain': (1.0, 0.6)}
    factors = {'L0_attn_Wq': 5.225,
     'L0_attn_Wk': 5.278,
     'L0_attn_Wv': 3.821,
     'L0_attn_Wo': 3.823,
     'L0_attn_pair_mix': 5.226,
     'L0_ffn_router_w': 5.579,
     'L0_ffn_w_gate': 4.892,
     'L0_ffn_w_up': 4.878,
     'L0_ffn_w_down': 4.878}
    for name, (base, spread) in spreads.items():
        noise = np.random.default_rng([zlib.crc32(name.encode()), seed]).standard_normal(out[name].shape)
        drawn = base * np.exp(spread * noise) if base else spread * noise
        out[name] = jnp.asarray(drawn.astype(out[name].dtype))
    for name, factor in factors.items():
        out[name] = (out[name] * factor).astype(out[name].dtype)
    return out
```

```python
from contextlib import ExitStack

import concourse.bass as bass
import numpy as np
from concourse import mybir

F32 = mybir.dt.float32
F32R = mybir.dt.float32r
BF16 = mybir.dt.bfloat16
I32 = mybir.dt.int32
U32 = mybir.dt.uint32
ALU = mybir.AluOpType
ACT = mybir.ActivationFunctionType
AX = mybir.AxisListType

P = 128
SEQS, SEQ = 16, 512
DIM, HEADS, KV, HD = 128, 16, 4, 8
J = HEADS // KV
WIN = 32
CH = P // WIN
TPS = SEQ // P
NT = SEQS * TPS
TOK = SEQS * SEQ
QF, KF = HEADS * HD, KV * HD
RF = QF + KF
PF = 2 * RF + KF
EXP, FF = 8, 256
CAP = TOK + P
SLACK = EXP * (P - 1) // P
NB = 2 * NT + SLACK + 1
JITTER = 2.0 * 0.01
RT_OPS = 17
SPARE = 8
ROWS = EXP * CAP + SPARE * P
CELLS = SEQS * EXP
U = 8
RMS_EPS, LN_EPS = 1e-6, 1e-5
NEG = -1.7e38
assert NB % U == 0 and KF == WIN and QF == P

(L_XHAT, L_PROJ, L_RMS, L_TR, L_KBD, L_SMAX, L_ST, L_PV, L_OUT) = (2, 3, 4, 5, 6, 7, 8, 9, 10)
(L_LN2, L_NB2, L_XN2, L_TX2, L_RT, L_RANK, L_SCAT) = (10, 11, 12, 13, 14, 15, 19)
PRO = 24
(B_LOAD, B_BT, B_GU, B_HT, B_DN, B_STORE) = (0, 2, 3, 4, 5, 6)
C_FIRST = 4


class At:

    def __init__(self, i, c):
        self.i, self.c = i, c

    def live(self, n):
        return not isinstance(self.i, int) or 0 <= U * self.i + self.c < n

    @property
    def n(self):
        return self.i * U + self.c

    def mod(self, m):
        return self.c % m

    def per(self, m):
        return self.i * (U // m) + self.c // m


def wait(eng, sem, value):
    if not isinstance(value, int) or value > 0:
        eng.wait_ge(sem, value)


def apart(eng, passed):
    eng.sem_inc(passed, 1)


def run(eng, chain, per, q, at=0):
    count = [at]

    def link(ins):
        count[0] += 1
        ins.then_inc(chain, 1)
        eng.wait_ge(chain, q * per + count[0])
    return link


def steps(eng, total, pro, end, body):
    for s in range(pro):
        body(lambda lag, s=s: At(s // U, s % U - lag))
    with eng.Fori(pro // U, end // U) as i:
        for u in range(U):
            body(lambda lag, u=u: At(i, u - lag))
    for s in range(end, total):
        body(lambda lag, s=s: At(s // U, s % U - lag))


def kernel_body(nc, x, w_proj, rope, gain, wo_self, wo_pair, mix_self, mix_pair, w_router,
                w_gu, w_dn, ident_in, ident16_in, kvmask_in, oneblk_in, smq_in, smk_in, stsel_in,
                stmask_in, tri_in, region_in, cells_in, out):
    xs_dram = nc.dram_tensor("expert_in", (ROWS, DIM), F32, kind="Internal").ap()
    ys_dram = nc.dram_tensor("expert_out", (NB * P, DIM), F32, kind="Internal").ap()
    v_dram = nc.dram_tensor("v_rows", (TOK, KF), F32, kind="Internal").ap()
    x_v = x.rearrange("(t p) d -> p t d", p=P)
    out_v = out.rearrange("(t p) d -> p t d", p=P)

    with ExitStack() as ctx:
        def sb(name, shape, dt=F32):
            return ctx.enter_context(nc.sbuf_tensor(name, shape, dt))

        def sem(name):
            return ctx.enter_context(nc.semaphore(name))

        wp = sb("wp", [P, PF])
        tab = sb("tab", [P, TPS, 2, RF])
        gn = sb("gn", [P, QF])
        wos, wop = sb("wos", [P, DIM]), sb("wop", [P, DIM])
        mixs, mixp = sb("mixs", [P, 1]), sb("mixp", [P, 1])
        wor, wo = sb("wor", [P, DIM]), sb("wo", [P, DIM])
        wr = sb("wr", [P, EXP])
        wgu = sb("wgu", [P, EXP, 2 * FF])
        wdn = sb("wdn", [P, EXP, 2, DIM])
        ident, ident16 = sb("ident", [P, P]), sb("ident16", [P, P], BF16)
        kvmask = sb("kvmask", [P, KV, WIN])
        oneblk = sb("oneblk", [P, KF])
        smq, smk = sb("smq", [P, P], BF16), sb("smk", [P, 2 * P], BF16)
        stsel = sb("stsel", [P, CH, P], BF16)
        stmov = sb("stmov", [P, 2, 2, P], BF16)
        tri = sb("tri", [P, 2, P], BF16)
        region = sb("region", [P, EXP])
        cells = sb("cells", [P, 2 * CELLS + 2 + EXP])
        zero = sb("zero", [P, DIM])

        xa = sb("xa", [P, NT, DIM])
        st1, mv1 = sb("st1", [P, TPS, 6]), sb("mv1", [P, 2, TPS, 2])
        ln1, rs1, nb1 = sb("ln1", [P, 2, TPS]), sb("rs1", [P, 2, TPS]), sb("nb1", [P, 2, TPS])
        st2, mv2 = sb("st2", [P, TPS, 6]), sb("mv2", [P, 2, TPS, 2])
        ln2, rs2, nb2 = sb("ln2", [P, 2, TPS]), sb("rs2", [P, 2, TPS]), sb("nb2", [P, 2, TPS])
        xh, xhT = sb("xh", [P, 4, DIM]), sb("xhT", [P, 4, P])
        sq, ss = sb("sq", [P, 4, RF]), sb("ss", [P, 4, RF // HD])
        lnr, rr = sb("lnr", [P, 4, RF // HD]), sb("rr", [P, 4, RF // HD])
        t1, t2, t3, t4 = (sb(f"t{n}", [P, 4, RF]) for n in range(1, 5))
        vtok, vext = sb("vtok", [P, 8, KF]), sb("vext", [P, 8, CH, KF])
        qk = sb("qk", [P, 4, QF + 2 * KF])
        kbd = sb("kbd", [P, 4, 2, KV, WIN])
        kbdr, qr = sb("kbdr", [P, 4, 2, KV, WIN], F32R), sb("qr", [P, 4, QF], F32R)
        mx, mm = sb("mx", [P, 2, CH * KV]), sb("mm", [P, 2, 2, CH * KV], BF16)
        pT = sb("pT", [P, 2, CH, 2 * P])
        nd, rec = sb("nd", [P, 2 * P]), sb("rec", [P, HEADS])
        y, yT = sb("y", [P, 2, QF]), sb("yT", [P, 2, P])
        xn2, xn2T = sb("xn2", [P, 8, DIM]), sb("xn2T", [P, TPS, P])
        lg, dd = sb("lg", [P, TPS, EXP]), sb("dd", [P, 2, TPS, EXP])
        ab, ff = sb("ab", [P, TPS, EXP]), sb("ff", [P, 2, TPS, EXP])
        m12, ee = sb("m12", [P, 2, TPS]), sb("ee", [P, 2, TPS, EXP])
        iw, mi = sb("iw", [P, TPS, EXP]), sb("mi", [P, TPS])
        oh, ms = sb("oh", [P, 2, 2, TPS, EXP]), sb("ms", [P, TPS, EXP])
        keep, sums = sb("keep", [P, 2, TPS, EXP]), sb("sums", [P, 2, TPS])
        both = sb("both", [P, 2, TPS, EXP], BF16)
        rk, prod, slotf = sb("rk", [P, TPS, EXP]), sb("prod", [P, 2, TPS, EXP]), sb("slotf", [P, 2, TPS])
        slot_r = sb("slot_r", [P, 2, 2, TPS], U32)
        slot_all = sb("slot_all", [P, SEQS, TPS * 2])
        w12 = sb("w12", [P, NT, 2])
        base = sb("base", [P, SEQS + 1, EXP])
        cnt, cnt_i, cb = sb("cnt", [P, CELLS]), sb("cnt_i", [P, CELLS], I32), sb("cb", [P, CELLS])
        start, nblk = sb("start", [P, CELLS]), sb("nblk", [P, CELLS])
        cum, low = ([sb(f"{name}{n}", [P, CELLS]) for n in range(2)] for name in ("cum", "low"))
        limits, shifts = sb("limits", [P, SEQS, 2 * EXP]), sb("shifts", [P, SEQS, 2 * EXP])
        jumps = sb("jumps", [P, SEQS, 2 * EXP])
        past = sb("past", [P, SEQS, 2 * TPS, 2 * EXP])
        row_all = sb("row_all", [P, NT, 2], U32)
        off, delta = sb("off", [P, CELLS + 1]), sb("delta", [P, CELLS])
        ind, cols = sb("ind", [P, 4, CELLS]), sb("cols", [P, 4])
        tabs, tail = sb("tabs", [1, 4, P], I32), sb("tail", [1, EXP], I32)
        xb, xbT = sb("xb", [P, 4, DIM]), sb("xbT", [P, 4, P])
        sil, h, hT = sb("sil", [P, 2, FF]), sb("h", [P, 4, FF]), sb("hT", [P, 4, FF])
        yb = sb("yb", [P, 4, DIM])
        ga = sb("ga", [P, 8, 2, DIM])
        acc, oo = sb("acc", [P, 2, DIM]), sb("oo", [P, 4, DIM])

        chb = ctx.enter_context(nc.psum_tensor("chb", [P, CH, 512], F32))
        pp, pv, tp, pm = (ctx.enter_context(nc.psum_tensor(n, [P, 512], F32))
                          for n in ("pp", "pv", "tp", "pm"))
        tp16 = tp[0:2 * CH * KV, P:P + P // 2].bitcast(BF16)
        LG, PREF, TOT = P, P + TPS * EXP, P + 2 * TPS * EXP

        c_attn, c_moe, c_mem, c_tab, c_zero = (sem(n) for n in (
            "const_attn", "const_moe", "const_mem", "const_tab", "const_zero"))
        passed = sem("passed")
        x_in, v_saved, v_in = sem("x_in"), sem("v_saved"), sem("v_in")
        chain, rt_chain, rk_chain, tb_chain = (sem(n) for n in ("dve_chain", "rt_chain", "rk_chain", "tb_chain"))
        rec_ok, mh_ok, acc_ok = sem("rec_ok"), sem("mh_ok"), sem("acc_ok")
        ln1_stats, act_ln, rstd1, nb1_ok = sem("ln1_stats"), sem("act_ln"), sem("rstd1"), sem("nb1_ok")
        ln2_stats, rstd2, nb2_ok = sem("ln2_stats"), sem("rstd2"), sem("nb2_ok")
        xh_ok, tx_done, xhT_ok, proj_done = sem("xh_ok"), sem("tx_done"), sem("xhT_ok"), sem("proj_done")
        sq_ok, v_ok, t12_ok, ss_ok, rms_ok = (sem(n) for n in ("sq_ok", "v_ok", "t12_ok", "ss_ok", "rms_ok"))
        t3_ok, t4_ok, tr_ok, kprev_ok = sem("t3_ok"), sem("t4_ok"), sem("tr_ok"), sem("kprev_ok")
        kbd_ok, kbdr_ok, qr_ok, smax_done = sem("kbd_ok"), sem("kbdr_ok"), sem("qr_ok"), sem("smax_done")
        max_ok, mm_ok, tm_done, stm_ok = sem("max_ok"), sem("mm_ok"), sem("tm_done"), sem("stm_ok")
        st_done, exp_ok, pv_done, nd_ok, y_ok = (sem(n) for n in ("st_done", "exp_ok", "pv_done", "nd_ok", "y_ok"))
        ty_done, yT_ok, wo_done, x2_ok = sem("ty_done"), sem("yT_ok"), sem("wo_done"), sem("x2_ok")
        xn2_ok, tx2_done, xn2T_ok, lg_done = sem("xn2_ok"), sem("tx2_done"), sem("xn2T_ok"), sem("lg_done")
        lg_read, dd_ok, ee_ok, both_ok = sem("lg_read"), sem("dd_ok"), sem("ee_ok"), sem("both_ok")
        rank_done, rank_read, slot_ok = sem("rank_done"), sem("rank_read"), sem("slot_ok")
        scat = [sem(f"scattered{n}") for n in range(2)]
        cols_ok, colsT_done, tabs_ok, tail_ok, tail_in = (sem(n) for n in (
            "cols_ok", "colsT_done", "tabs_ok", "tail_ok", "tail_in"))
        xb_in = [sem(f"xb_in{n}") for n in range(4)]
        yb_out = [sem(f"yb_out{n}") for n in range(4)]
        bt_done, xbT_ok, gu_done, sil_ok, h_ok = (sem(n) for n in ("bt_done", "xbT_ok", "gu_done", "sil_ok", "h_ok"))
        ht_done, hT_ok, dn_done, yb_ok = sem("ht_done"), sem("hT_ok"), sem("dn_done"), sem("yb_ok")
        limits_ok, row_chain, comb_ok = sem("limits_ok"), sem("row_chain"), sem("comb_ok")
        gath = [sem(f"gathered{n}") for n in range(2 * TPS)]
        stored = [sem(f"stored{n}") for n in range(2)]

        tabs_flat = tabs[:, :, :].rearrange("a b c -> a (b c)")
        bt_ps, dn_ps = (tp, pm), (pp, pv)

        block = ctx.enter_context(nc.Block())

        @block.sync
        def _(sp):
            def load_x(q):
                sp.dma_start(xa[:, bass.ds(q * TPS, TPS), :],
                             x_v[:, bass.ds(q * TPS, TPS), :]).then_inc(x_in, 16)

            def values(q, par, after):
                wait(sp, v_ok, (q + 1) * TPS)
                apart(sp, passed)
                sp.dma_start(v_dram[bass.ds(q * SEQ, SEQ), :].rearrange("(t p) f -> p t f", p=P),
                             vtok[:, par * TPS:(par + 1) * TPS, :]).then_inc(v_saved, 16)
                sp.wait_ge(v_saved, (q + 1) * 16)
                apart(sp, passed)
                if after:
                    wait(sp, pv_done, (q - 1) * TPS)
                    apart(sp, passed)
                src = v_dram[bass.ds(q * SEQ, SEQ), :].rearrange("(t c k) f -> k t c f", c=CH, k=WIN)
                for g in range(KV):
                    sp.dma_start(vext[g * WIN:(g + 1) * WIN, par * TPS:(par + 1) * TPS, :, g * HD:(g + 1) * HD],
                                 src[:, :, :, g * HD:(g + 1) * HD]).then_inc(v_in, 16)

            for q in range(4):
                load_x(q)
                sp.wait_ge(x_in, (q + 1) * 16)
            sp.wait_ge(c_mem, 1)
            for n in range(SPARE):
                sp.dma_start(xs_dram[EXP * CAP + n * P:EXP * CAP + (n + 1) * P, :], zero[:, :]).then_inc(c_zero, 16)
            values(0, 0, False)
            values(1, 1, False)
            with sp.Fori(1, SEQS // 2 - 1) as i:
                for par in range(2):
                    load_x(i * 2 + par + 2)
                    values(i * 2 + par, par, True)
                    sp.wait_ge(x_in, (i * 2 + par + 3) * 16)
                    apart(sp, passed)
            for par in range(2):
                values(SEQS - 2 + par, par, True)
            sp.wait_ge(tail_ok, 1)
            for e in range(EXP):
                at = sp.value_load(tail[0:1, e:e + 1], min_val=0, max_val=EXP * CAP)
                sp.dma_start(xs_dram[bass.ds(at, P), :], zero[:, :]).then_inc(tail_in, 16)
            sp.wait_ge(tail_in, EXP * 16)
            sp.wait_ge(c_zero, SPARE * 16)
            for n in range(2):
                sp.wait_ge(scat[n], NT * 16)
            sp.wait_ge(tabs_ok, 1)

            def addr(b):
                return sp.value_load(tabs_flat[0:1, bass.ds(b, 1)], min_val=0, max_val=ROWS - P)

            def load(b):
                at = addr(b.n)
                wait(sp, bt_done, b.n - 3)
                sp.dma_start(xb[:, b.mod(4), :], xs_dram[bass.ds(at, P), :])\
                  .then_inc(xb_in[b.mod(4)], 16)

            def store(b):
                sp.wait_ge(yb_ok, b.n + 1)
                sp.dma_start(ys_dram[bass.ds(b.n * P, P), :], yb[:, b.mod(4), :])\
                  .then_inc(yb_out[b.mod(4)], 16)

            def slot(at, only=None):
                b = at(B_LOAD)
                if b.live(NB):
                    load(b)
                b = at(B_STORE)
                if b.live(NB):
                    store(b)

            def store_out(k, par):
                sp.wait_ge(comb_ok, k + 2)
                apart(sp, passed)
                sp.dma_start(out_v[:, bass.ds(k, 2), :], oo[:, 2 * par:2 * par + 2, :])\
                  .then_inc(stored[par], 16)

            def turn(i, first=None, second=None):
                for u in range(U):
                    slot(lambda lag, u=u: At(i, u - lag))
                    if u == 2 and second is not None:
                        store_out(second * TPS + 2, 1)
                    if u == 6 and first is not None:
                        store_out(first * TPS, 0)

            turn(0)
            with sp.Fori(1, C_FIRST) as i:
                turn(i)
            turn(C_FIRST, 0)
            with sp.Fori(C_FIRST + 1, NB // U) as i:
                turn(i, i - C_FIRST, i - C_FIRST - 1)
            for s in range(NB, NB + B_STORE):
                slot(lambda lag, s=s: At(s // U, s % U - lag))
            in_b = NB // U - C_FIRST
            store_out((in_b - 1) * TPS + 2, 1)
            with sp.Fori(in_b, SEQS) as m:
                for par in range(2):
                    store_out(m * TPS + 2 * par, par)
            for n in range(2):
                sp.wait_ge(stored[n], NT // 4 * 16)

        @block.scalar
        def _(act):
            for dst, src in ((ident, ident_in), (wp, w_proj), (tab, rope), (gn, gain), (wos, wo_self),
                             (wop, wo_pair), (mixs, mix_self), (mixp, mix_pair), (wr, w_router),
                             (ident16, ident16_in), (kvmask, kvmask_in), (oneblk, oneblk_in),
                             (smq, smq_in), (smk, smk_in), (stsel, stsel_in), (tri, tri_in),
                             (region, region_in), (cells, cells_in)):
                act.dma_start(dst[:], src).then_inc(c_attn, 16)
            for r in range(2):
                act.dma_start(stmov[2 * CH * KV:P, r, :, :], stmask_in).then_inc(c_attn, 16)
            act.dma_start(wgu[:, :, :], w_gu).then_inc(c_moe, 16)
            act.dma_start(wdn[:, :, :, :], w_dn).then_inc(c_moe, 16)
            act.preload_act_table_set("natural_log_exp_and_others")

            def step(at):
                t = at(L_PROJ)
                if t.live(NT):
                    act.wait_ge(tx_done, t.n + 1)
                    wait(act, proj_done, t.n - 3)
                    nc.scalar.copy(xhT[:, t.mod(4), :], tp[:, 0:P]).then_inc(xhT_ok, 1)
                t = at(L_RMS)
                if t.live(NT):
                    r = t.mod(4)
                    act.wait_ge(ss_ok, t.n + 1)
                    nc.scalar.activation(lnr[:, r, :], ss[:, r, :], ACT.Ln, bias=HD * RMS_EPS).then_inc(act_ln, 1)
                    act.wait_ge(act_ln, t.n + 1)
                    wait(act, t4_ok, t.n - 3)
                    nc.scalar.activation(rr[:, r, :], lnr[:, r, :], ACT.Exp, scale=-0.5).then_inc(rms_ok, 1)
                t = at(L_TR)
                if t.live(NT):
                    r = t.mod(4)
                    act.wait_ge(tr_ok, t.n + 1)
                    if r > 0:
                        nc.scalar.copy(qk[0:WIN, r, RF:RF + KF], qk[P - WIN:P, r - 1, QF:RF])
                    for c in range(CH - 1):
                        last = nc.scalar.copy(qk[(c + 1) * WIN:(c + 2) * WIN, r, RF:RF + KF],
                                              qk[c * WIN:(c + 1) * WIN, r, QF:RF])
                    last.then_inc(kprev_ok, 1)
                t = at(L_KBD)
                if t.live(NT):
                    act.wait_ge(tr_ok, t.n + 1)
                    wait(act, smax_done, t.n - 3)
                    nc.scalar.copy(qr[:, t.mod(4), :], qk[:, t.mod(4), 0:QF]).then_inc(qr_ok, 1)
                t = at(L_PROJ)
                if t.live(NT):
                    act.wait_ge(proj_done, t.n + 1)
                    wait(act, ss_ok, t.n - 3)
                    nc.scalar.activation(sq[:, t.mod(4), :], pp[:, 0:RF], ACT.Square).then_inc(sq_ok, 1)
                    if t.mod(4) == 0:
                        wait(act, v_saved, (t.per(4) - 1) * 16)
                    nc.scalar.copy(vtok[:, t.mod(8), :], pp[:, 2 * RF:PF]).then_inc(v_ok, 1)
                t = at(L_XHAT)
                if t.live(NT):
                    v, par = t.mod(4), t.mod(8) // 4
                    act.wait_ge(nb1_ok, t.per(4) + 1)
                    wait(act, tx_done, t.n - 3)
                    nc.scalar.activation(xh[:, v, :], xa[:, t.n, :], ACT.Identity, scale=rs1[:, par, v:v + 1],
                                         bias=nb1[:, par, v:v + 1]).then_inc(xh_ok, 1)
                t = at(L_OUT)
                if t.live(NT):
                    act.wait_ge(ty_done, t.n + 1)
                    wait(act, wo_done, t.n - 1)
                    nc.scalar.copy(yT[:, t.mod(2), :], tp[:, 2 * P:3 * P]).then_inc(yT_ok, 1)
                t = at(L_RT)
                if t.live(NT) and t.mod(4) == 3:
                    act.wait_ge(dd_ok, t.per(4) + 1)
                    nc.scalar.activation(ee[:, :, :, :], dd[:, :, :, :], ACT.Exp).then_inc(ee_ok, 1)
                for lag, u, stats, mv, ln, rs, done in ((1, 0, ln1_stats, mv1, ln1, rs1, rstd1),
                                                        (L_NB2, 3, ln2_stats, mv2, ln2, rs2, rstd2)):
                    t = at(lag)
                    if t.live(NT) and t.mod(4) == u:
                        par, q = t.mod(8) // 4, t.per(4)
                        act.wait_ge(stats, 2 * (q + 1))
                        nc.scalar.activation(ln[:, par, :], mv[:, par, :, 1], ACT.Ln, bias=LN_EPS).then_inc(done, 1)
                        act.wait_ge(done, 2 * q + 1)
                        nc.scalar.activation(rs[:, par, :], ln[:, par, :], ACT.Exp, scale=-0.5).then_inc(done, 1)
                t = at(L_ST)
                if t.live(NT):
                    r = t.mod(2)
                    act.wait_ge(st_done, t.n + 1)
                    wait(act, pv_done, t.n - 1)
                    if t.mod(4) == 0:
                        nc.scalar.activation(pT[:, r, 0, 0:P], chb[:, 0, 0:P], ACT.Exp)
                        nc.scalar.activation(pT[:, r, 1, :], chb[:, 1, 0:2 * P], ACT.Exp)
                    else:
                        nc.scalar.activation(pT[:, r, 0:2, :], chb[:, 0:2, 0:2 * P], ACT.Exp)
                    nc.scalar.activation(pT[:, r, 2:4, :], chb[:, 2:4, 0:2 * P], ACT.Exp).then_inc(exp_ok, 1)
                t = at(L_SMAX)
                if t.live(NT):
                    act.wait_ge(tm_done, t.n + 1)
                    wait(act, st_done, t.n - 1)
                    nc.scalar.copy(stmov[0:2 * CH * KV, t.mod(2), :, :],
                                   tp16.unsqueeze(1).to_broadcast([2 * CH * KV, 2, P])).then_inc(stm_ok, 1)
                t = at(L_XN2)
                if t.live(NT) and t.mod(4) == 3:
                    par = t.mod(8) // 4
                    act.wait_ge(nb2_ok, t.per(4) + 1)
                    wait(act, scat[par], t.per(8) * 2 * TPS * 16)
                    for v in range(TPS):
                        last = nc.scalar.activation(xn2[:, TPS * par + v, :], xa[:, t.n - 3 + v, :], ACT.Identity,
                                                    scale=rs2[:, par, v:v + 1], bias=nb2[:, par, v:v + 1])
                    last.then_inc(xn2_ok, 1)
                t = at(L_TX2)
                if t.live(NT) and t.mod(4) == 3:
                    act.wait_ge(tx2_done, t.per(4) + 1)
                    wait(act, lg_done, t.per(4))
                    nc.scalar.copy(xn2T[:, :, :], tp[:, :].rearrange("p (v n) -> p v n", v=TPS)).then_inc(xn2T_ok, 1)

            act.wait_ge(c_mem, 1)
            steps(act, NT + L_SCAT + 1, PRO, NT, step)

            def slot(at):
                b = at(B_BT)
                if b.live(NB):
                    act.wait_ge(bt_done, b.n + 1)
                    wait(act, gu_done, b.n - 3)
                    nc.scalar.copy(xbT[:, b.mod(4), :], bt_ps[b.mod(2)][:, 0:P]).then_inc(xbT_ok, 1)
                b = at(B_HT)
                if b.live(NB):
                    act.wait_ge(ht_done, b.n + 1)
                    wait(act, dn_done, b.n - 3)
                    nc.scalar.copy(hT[:, b.mod(4), :], chb[:, 2 + b.mod(2), 0:FF]).then_inc(hT_ok, 1)
                b = at(B_GU)
                if b.live(NB):
                    act.wait_ge(gu_done, b.n + 1)
                    wait(act, h_ok, b.n - 1)
                    nc.scalar.activation(sil[:, b.mod(2), :], chb[:, b.mod(2), 0:FF], ACT.Silu).then_inc(sil_ok, 1)

            act.preload_act_table_set("silu_and_others")
            steps(act, NB + B_STORE, U, NB, slot)

        @block.tensor
        def _(pe):
            pe.wait_ge(c_attn, 20 * 16)
            pe.wait_ge(c_mem, 3)

            def step(at):
                t = at(L_PROJ)
                if t.live(NT):
                    pe.wait_ge(xh_ok, t.n + 1)
                    b = at(L_SMAX + 1)
                    if b.live(NT):
                        pe.wait_ge(stm_ok, b.n + 1)
                    nc.tensor.transpose(tp[:, 0:P], xh[:, t.mod(4), :], ident[:, :]).then_inc(tx_done, 1)
                t = at(L_SMAX)
                if t.live(NT):
                    r = t.mod(4)
                    pe.wait_ge(kbdr_ok, t.n + 1)
                    pe.wait_ge(qr_ok, t.n + 1)
                    wait(pe, exp_ok, t.n - 1)
                    width = [P if r == 0 and c == 0 else 2 * P for c in range(CH)]
                    for c in range(CH):
                        nc.tensor.matmul(chb[:, c, 0:width[c]], smq[:, :], smk[:, 0:width[c]], start=True, stop=False)
                    for c in range(CH):
                        rows = slice(c * WIN, (c + 1) * WIN)
                        k = kbdr[rows, r, :, :, :].rearrange("p a b c -> p (a b c)")
                        last = nc.tensor.matmul(chb[:, c, 0:width[c]], qr[rows, r, :], k[:, 0:width[c]],
                                                start=False, stop=True)
                    last.then_inc(smax_done, 1)
                t = at(L_RANK)
                if t.live(NT) and t.mod(4) == 3:
                    pe.wait_ge(both_ok, t.per(4) + 1)
                    b = at(L_OUT + 1)
                    if b.live(NT):
                        pe.wait_ge(x2_ok, b.n + 1)
                    pref = pm[:, PREF:PREF + TPS * EXP].rearrange("p (v e) -> p v e", v=TPS)
                    m = both[:, t.mod(8) // 4, :, :]
                    nc.tensor.matmul(pm[:, PREF:PREF + TPS * EXP], tri[:, 0, :], m.rearrange("p v e -> p (v e)"),
                                     start=True, stop=False, skip_group_check=True)
                    for v in range(TPS - 1):
                        n = TPS - 1 - v
                        nc.tensor.matmul(pref[:, v + 1:TPS, :], tri[:, 1, :],
                                         m[:, v, :].unsqueeze(1).to_broadcast([P, n, EXP]),
                                         start=False, stop=(v == TPS - 2), skip_group_check=True)
                    for v in range(TPS):
                        last = nc.tensor.matmul(pm[:, TOT:TOT + EXP], tri[:, 1, :], m[:, v, :], start=False,
                                                stop=(v == TPS - 1), skip_group_check=True)
                    last.then_inc(rank_done, 1)
                t = at(L_PROJ)
                if t.live(NT):
                    pe.wait_ge(xhT_ok, t.n + 1)
                    wait(pe, t12_ok, t.n)
                    nc.tensor.matmul(pp[:, 0:PF], xhT[:, t.mod(4), :], wp[:, :], start=True, stop=True)\
                      .then_inc(proj_done, 1)
                t = at(L_OUT)
                if t.live(NT):
                    pe.wait_ge(y_ok, t.n + 1)
                    b = at(L_PROJ)
                    if b.live(NT):
                        pe.wait_ge(xhT_ok, b.n + 1)
                    else:
                        b = at(L_SMAX + 1)
                        if b.live(NT):
                            pe.wait_ge(stm_ok, b.n + 1)
                    nc.tensor.transpose(tp[:, 2 * P:3 * P], y[:, t.mod(2), :], ident[:, :]).then_inc(ty_done, 1)
                t = at(L_ST)
                if t.live(NT):
                    r = t.mod(4)
                    pe.wait_ge(stm_ok, t.n + 1)
                    pe.wait_ge(kbd_ok, t.n + 1)
                    b = at(L_SMAX)
                    if b.live(NT):
                        pe.wait_ge(max_ok, b.n + 1)
                    mov = stmov[:, t.mod(2), :, :].rearrange("p a b -> p (a b)")
                    k = kbd[:, r, :, :, :].rearrange("p a b c -> p a (b c)")
                    for c in range(CH):
                        w = P if r == 0 and c == 0 else 2 * P
                        nc.tensor.matmul(chb[:, c, 0:w], stsel[:, c, :], mov[:, 0:w], start=True, stop=False)
                    for half in range(2):
                        for c in range(CH):
                            if half == 1 and c == 0 and r == 0:
                                continue
                            rows = slice(c * WIN, (c + 1) * WIN)
                            last = nc.tensor.matmul(chb[:, c, half * P:(half + 1) * P], k[rows, half, :],
                                                    qk[rows, r, 0:QF], start=False,
                                                    stop=(half == 1 or (c == 0 and r == 0)))
                    last.then_inc(st_done, 1)
                t = at(L_OUT)
                if t.live(NT):
                    pe.wait_ge(yT_ok, t.n + 1)
                    b = at(L_RANK)
                    if b.live(NT) and b.mod(4) == 3:
                        pe.wait_ge(rank_read, b.per(4) + 1)
                    b = at(L_RT)
                    if b.live(NT) and b.mod(4) == 3:
                        pe.wait_ge(lg_read, b.per(4) + 1)
                    nc.tensor.matmul(pm[:, 0:DIM], yT[:, t.mod(2), :], wo[:, :], start=True, stop=True)\
                      .then_inc(wo_done, 1)
                t = at(L_SMAX)
                if t.live(NT):
                    pe.wait_ge(mm_ok, t.n + 1)
                    b = at(L_OUT)
                    if b.live(NT):
                        pe.wait_ge(yT_ok, b.n + 1)
                    nc.tensor.transpose(tp16, mm[:, t.mod(2), :, :].rearrange("p a b -> p (a b)"), ident16[:, :])\
                      .then_inc(tm_done, 1)
                t = at(L_PV)
                if t.live(NT):
                    r = t.mod(8)
                    pe.wait_ge(exp_ok, t.n + 1)
                    pe.wait_ge(v_in, (t.per(4) + 1) * KV * 16)
                    wait(pe, nd_ok, t.n)
                    for what in range(2):
                        for half in range(2):
                            for c in range(CH):
                                first = t.mod(4) == 0 and c == 0
                                if half == 1 and first:
                                    continue
                                if what == 1:
                                    lhs = oneblk[:, :]
                                elif half == 0:
                                    lhs = vext[:, r, c, :]
                                else:
                                    lhs = vext[:, r, c - 1, :] if c else vext[:, r - 1, CH - 1, :]
                                last = nc.tensor.matmul(pv[c * WIN:(c + 1) * WIN, what * P:(what + 1) * P], lhs,
                                                        pT[:, t.mod(2), c, half * P:(half + 1) * P],
                                                        start=(half == 0), stop=(half == 1 or first),
                                                        tile_position=(0, c * WIN))
                    last.then_inc(pv_done, 1)
                t = at(L_TX2)
                if t.live(NT) and t.mod(4) == 3:
                    par = t.mod(8) // 4
                    pe.wait_ge(xn2_ok, t.per(4) + 1)
                    b = at(L_SMAX)
                    if b.live(NT):
                        pe.wait_ge(stm_ok, b.n + 1)
                    b = at(L_OUT)
                    if b.live(NT):
                        pe.wait_ge(yT_ok, b.n + 1)
                    for v in range(TPS):
                        last = nc.tensor.transpose(tp[:, v * P:(v + 1) * P], xn2[:, TPS * par + v, :], ident[:, :])
                    last.then_inc(tx2_done, 1)
                    pe.wait_ge(xn2T_ok, t.per(4) + 1)
                    if b.live(NT):
                        pe.wait_ge(x2_ok, b.n + 1)
                    for v in range(TPS):
                        last = nc.tensor.matmul(pm[:, LG + v * EXP:LG + (v + 1) * EXP], xn2T[:, v, :], wr[:, :],
                                                start=True, stop=True)
                    last.then_inc(lg_done, 1)

            steps(pe, NT + L_SCAT + 1, PRO, NT, step)

            pe.wait_ge(cols_ok, 1)
            for n in range(4):
                last = nc.tensor.transpose(pm[0:1, n * P:(n + 1) * P], cols[:, n:n + 1], ident[:, :])
            last.then_inc(colsT_done, 1)
            pe.wait_ge(tabs_ok, 1)
            pe.wait_ge(c_moe, 32)

            def expert(b):
                return pe.value_load(tabs_flat[0:1, bass.ds(b.n + 2 * P, 1)], min_val=0, max_val=EXP - 1)

            def slot(at):
                b = at(B_GU)
                if b.live(NB):
                    e = expert(b)
                    pe.wait_ge(xbT_ok, b.n + 1)
                    wait(pe, h_ok, b.n - 1)
                    nc.tensor.matmul(chb[:, b.mod(2), :], xbT[:, b.mod(4), :], wgu[:, e, :],
                                     start=True, stop=True).then_inc(gu_done, 1)
                b = at(B_HT)
                if b.live(NB):
                    pe.wait_ge(h_ok, b.n + 1)
                    wait(pe, hT_ok, b.n - 1)
                    for k in range(2):
                        last = nc.tensor.transpose(chb[:, 2 + b.mod(2), k * P:(k + 1) * P],
                                                   h[:, b.mod(4), k * P:(k + 1) * P], ident[:, :])
                    last.then_inc(ht_done, 1)
                b = at(B_BT)
                if b.live(NB):
                    pe.wait_ge(xb_in[b.mod(4)], (b.per(4) + 1) * 16)
                    wait(pe, xbT_ok, b.n - 1)
                    nc.tensor.transpose(bt_ps[b.mod(2)][:, 0:P], xb[:, b.mod(4), :], ident[:, :]).then_inc(bt_done, 1)
                b = at(B_DN)
                if b.live(NB):
                    e = expert(b)
                    pe.wait_ge(hT_ok, b.n + 1)
                    wait(pe, yb_ok, b.n - 1)
                    for k in range(2):
                        last = nc.tensor.matmul(dn_ps[b.mod(2)][:, 0:DIM], hT[:, b.mod(4), k * P:(k + 1) * P],
                                                wdn[:, e, k, :], start=(k == 0), stop=(k == 1))
                    last.then_inc(dn_done, 1)

            steps(pe, NB + B_STORE, U, NB, slot)

        @block.vector
        def _(dve):
            nc.vector.memset(qk[:, :, :], 0.0).then_inc(chain, 1)
            nc.vector.memset(zero[:, :], 0.0).then_inc(chain, 1)
            dve.wait_ge(chain, 2)
            nc.vector.memset(vext[:, :, :, :], 0.0).then_inc(c_mem, 1)
            dve.wait_ge(c_attn, 20 * 16)
            for u in range(TPS):
                for n in range(2):
                    nc.vector.tensor_tensor(tab[:, u, n, 0:QF], tab[:, u, n, 0:QF], gn[:, :], ALU.mult)
            nc.vector.tensor_copy(base[:, 0, :], region[:, :])
            nc.vector.tensor_scalar(wor[:, :], wop[:, :], mixp[:, 0:1], None, ALU.mult).then_inc(c_mem, 1)
            dve.wait_ge(c_mem, 2)
            nc.vector.scalar_tensor_tensor(out=wo[:, :], in0=wos[:, :], scalar=mixs[:, 0:1], in1=wor[:, :],
                                           op0=ALU.mult, op1=ALU.add).then_inc(c_mem, 1)

            def stats(st, mv, t0, par, done, q):
                for v in range(TPS):
                    last = nc.vector.bn_stats(st[:, v, :], xa[:, t0 + v, :])
                last.then_inc(done, 1)
                dve.wait_ge(done, 2 * q + 1)
                apart(dve, passed)
                for v in range(TPS):
                    last = nc.vector.bn_aggr(mv[:, par, v, :], st[:, v, :])
                last.then_inc(done, 1)

            first_slot = cells[:, 0:CELLS]
            step_expert = cells[:, CELLS:2 * CELLS]
            block_no = cells[:, 2 * CELLS:2 * CELLS + 2]
            order = cells[:, 2 * CELLS + 2:]

            def over_experts(a):
                return a.unsqueeze(2).to_broadcast([P, TPS, EXP])

            def one_hot(link, k, par):
                link(nc.vector.scalar_tensor_tensor(
                    out=iw[:, :, :], in0=dd[:, k, :, :], scalar=0.0,
                    in1=order.unsqueeze(1).to_broadcast([P, TPS, EXP]), op0=ALU.is_ge, op1=ALU.mult))
                link(nc.vector.tensor_reduce(mi[:, :], iw[:, :, :], AX.X, ALU.max))
                link(nc.vector.tensor_tensor(oh[:, par, k, :, :], iw[:, :, :], over_experts(mi[:, :]), ALU.is_equal))

            def choose(t):
                q, par = t.per(4), t.mod(8) // 4
                link = run(dve, rt_chain, RT_OPS, q)
                dve.wait_ge(lg_done, q + 1)
                nc.vector.tensor_copy(lg[:, :, :].rearrange("p v e -> p (v e)"), pm[:, LG:LG + TPS * EXP])\
                  .then_inc(lg_read, 1)
                dve.wait_ge(lg_read, q + 1)
                link(nc.vector.scalar_tensor_tensor(out=ab[:, :, :], in0=lg[:, :, :], scalar=-1.0,
                                                    in1=lg[:, :, :], op0=ALU.mult, op1=ALU.max))
                link(nc.vector.tensor_reduce(m12[:, 0, :], lg[:, :, :], AX.X, ALU.max))
                link(nc.vector.tensor_tensor(dd[:, 0, :, :], lg[:, :, :], over_experts(m12[:, 0, :]), ALU.subtract))
                one_hot(link, 0, par)
                link(nc.vector.scalar_tensor_tensor(out=ms[:, :, :], in0=oh[:, par, 0, :, :], scalar=NEG,
                                                    in1=lg[:, :, :], op0=ALU.mult, op1=ALU.add))
                link(nc.vector.tensor_reduce(m12[:, 1, :], ms[:, :, :], AX.X, ALU.max))
                wait(dve, ee_ok, q)
                nc.vector.tensor_tensor(dd[:, 1, :, :], ms[:, :, :], over_experts(m12[:, 1, :]), ALU.subtract)\
                  .then_inc(dd_ok, 1)
                dve.wait_ge(dd_ok, q + 1)
                one_hot(link, 1, par)
                for k in range(2):
                    link(nc.vector.tensor_tensor(ff[:, k, :, :], ab[:, :, :], over_experts(m12[:, k, :]), ALU.max))
                link(nc.vector.scalar_tensor_tensor(out=ff[:, :, :, :], in0=ff[:, :, :, :], scalar=JITTER,
                                                    in1=dd[:, :, :, :], op0=ALU.mult, op1=ALU.add))

            def weigh(t):
                q, par = t.per(4), t.mod(8) // 4
                link = run(dve, rt_chain, RT_OPS, q, RT_OPS - 3)
                dve.wait_ge(ee_ok, q + 1)
                link(nc.vector.scalar_tensor_tensor(out=keep[:, :, :, :], in0=ff[:, :, :, :], scalar=0.0,
                                                    in1=ee[:, :, :, :], op0=ALU.is_ge, op1=ALU.mult))
                link(nc.vector.tensor_reduce(sums[:, :, :], keep[:, :, :, :], AX.X, ALU.add))
                link(nc.vector.reciprocal(w12[:, bass.ds(t.n - 3, TPS), :].rearrange("p v k -> p k v"), sums[:, :, :]))
                wait(dve, rank_done, q - 1)
                nc.vector.tensor_tensor(both[:, par, :, :], oh[:, par, 0, :, :], oh[:, par, 1, :, :], ALU.add)\
                  .then_inc(both_ok, 1)

            def slots(t):
                q, par = t.per(4), t.mod(8) // 4
                link = run(dve, rk_chain, 3, q)
                dve.wait_ge(rank_done, q + 1)
                nc.vector.tensor_tensor(base[:, q + 1, :], base[:, q, :], pm[:, TOT:TOT + EXP], ALU.add)
                nc.vector.tensor_tensor(rk[:, :, :], pm[:, PREF:PREF + TPS * EXP].rearrange("p (v e) -> p v e", v=TPS),
                                        base[:, q, :].unsqueeze(1).to_broadcast([P, TPS, EXP]), ALU.add)\
                  .then_inc(rank_read, 1)
                dve.wait_ge(rank_read, q + 1)
                link(nc.vector.tensor_tensor(prod[:, :, :, :], oh[:, par, :, :, :],
                                             rk[:, :, :].unsqueeze(1).to_broadcast([P, 2, TPS, EXP]), ALU.mult))
                link(nc.vector.tensor_reduce(slotf[:, :, :], prod[:, :, :, :], AX.X, ALU.add))
                link(nc.vector.tensor_copy(slot_all[:, q, :].rearrange("p (v k) -> p k v", k=2), slotf[:, :, :]))
                wait(dve, scat[par], t.per(8) * 2 * TPS * 16)
                nc.vector.tensor_copy(slot_r[:, par, :, :], slotf[:, :, :]).then_inc(slot_ok, 1)

            def step(at):
                t = at(L_OUT)
                if t.live(NT):
                    dve.wait_ge(pv_done, t.n + 1)
                    nc.vector.transpose(nd[:, :], pv[:, 0:2 * P]).then_inc(nd_ok, 1)
                    dve.wait_ge(nd_ok, t.n + 1)
                    nc.vector.reciprocal(rec[:, :], nd[:, P:2 * P].rearrange("p (h d) -> p h d", d=HD)[:, :, 0])\
                      .then_inc(rec_ok, 1)
                    dve.wait_ge(rec_ok, t.n + 1)
                    wait(dve, ty_done, t.n - 1)
                    nc.vector.tensor_tensor(y[:, t.mod(2), :].rearrange("p (h d) -> p h d", d=HD),
                                            nd[:, 0:P].rearrange("p (h d) -> p h d", d=HD),
                                            rec[:, :].unsqueeze(2).to_broadcast([P, HEADS, HD]), ALU.mult)\
                      .then_inc(y_ok, 1)
                t = at(L_RT)
                if t.live(NT) and t.mod(4) == 3:
                    choose(t)
                t = at(L_SMAX)
                if t.live(NT):
                    r = t.mod(2)
                    dve.wait_ge(smax_done, t.n + 1)

                    def chunk_max(c0, c1, halves):
                        src = chb[:, c0:c1, 0:halves * P].rearrange("p c (h g k) -> p c g h k", h=halves, g=KV)
                        dst = mx[:, r, c0 * KV:c1 * KV].rearrange("p (c g) -> p c g", g=KV)
                        return nc.vector.tensor_reduce(dst, src, AX.XY, ALU.max)

                    if t.mod(4) == 0:
                        chunk_max(0, 1, 1)
                        chunk_max(1, 2, 2)
                    else:
                        chunk_max(0, 2, 2)
                    chunk_max(2, 4, 2).then_inc(max_ok, 1)
                    dve.wait_ge(max_ok, t.n + 1)
                    wait(dve, tm_done, t.n - 1)
                    nc.vector.tensor_scalar(mm[:, r, 0, :], mx[:, r, :], -1.0, None, ALU.mult).then_inc(mh_ok, 1)
                    dve.wait_ge(mh_ok, t.n + 1)
                    nc.vector.scalar_tensor_tensor(out=mm[:, r, 1, :], in0=mx[:, r, :], scalar=-1.0,
                                                   in1=mm[:, r, 0, :], op0=ALU.mult, op1=ALU.subtract)\
                      .then_inc(mm_ok, 1)
                t = at(L_RANK)
                if t.live(NT) and t.mod(4) == 3:
                    slots(t)
                t = at(L_TR)
                if t.live(NT):
                    dve.wait_ge(t4_ok, t.n + 1)
                    wait(dve, st_done, t.n - 3)
                    wait(dve, kprev_ok, t.n - 2)
                    nc.vector.transpose(qk[:, t.mod(4), 0:RF], t4[:, t.mod(4), :]).then_inc(tr_ok, 1)
                t = at(L_KBD)
                if t.live(NT):
                    dve.wait_ge(kprev_ok, t.n + 1)
                    nc.vector.tensor_tensor(
                        kbd[:, t.mod(4), :, :, :],
                        qk[:, t.mod(4), QF:QF + 2 * KF].rearrange("p (h k) -> p h k", h=2).unsqueeze(2)
                        .to_broadcast([P, 2, KV, WIN]),
                        kvmask[:, :, :].unsqueeze(1).to_broadcast([P, 2, KV, WIN]), ALU.mult).then_inc(kbd_ok, 1)
                t = at(L_PROJ)
                if t.live(NT):
                    r = t.mod(4)
                    dve.wait_ge(v_ok, t.n + 1)
                    wait(dve, t3_ok, t.n - 3)
                    nc.vector.tensor_tensor(t1[:, r, :], pp[:, 0:RF], tab[:, r, 0, :], ALU.mult)
                    nc.vector.tensor_tensor(t2[:, r, :], pp[:, RF:2 * RF], tab[:, r, 1, :], ALU.mult)\
                      .then_inc(t12_ok, 1)
                    dve.wait_ge(sq_ok, t.n + 1)
                    wait(dve, rms_ok, t.n - 3)
                    nc.vector.tensor_reduce(ss[:, r, :], sq[:, r, :].rearrange("p (h d) -> p h d", d=HD),
                                            AX.X, ALU.add).then_inc(ss_ok, 1)
                t = at(0)
                if t.live(NT) and t.mod(4) == 0:
                    dve.wait_ge(x_in, (t.per(4) + 1) * 16)
                    stats(st1, mv1, t.n, t.mod(8) // 4, ln1_stats, t.per(4))
                for lag, u, mv, rs, nb, ready, done in ((1, 0, mv1, rs1, nb1, rstd1, nb1_ok),
                                                        (L_NB2, 3, mv2, rs2, nb2, rstd2, nb2_ok)):
                    t = at(lag)
                    if t.live(NT) and t.mod(4) == u:
                        par = t.mod(8) // 4
                        dve.wait_ge(ready, 2 * (t.per(4) + 1))
                        nc.vector.scalar_tensor_tensor(out=nb[:, par, :], in0=mv[:, par, :, 0], scalar=-1.0,
                                                       in1=rs[:, par, :], op0=ALU.mult, op1=ALU.mult).then_inc(done, 1)
                t = at(L_OUT)
                if t.live(NT):
                    dve.wait_ge(wo_done, t.n + 1)
                    nc.vector.tensor_tensor(xa[:, t.n, :], xa[:, t.n, :], pm[:, 0:DIM], ALU.add).then_inc(x2_ok, 1)
                    if t.mod(4) == 3:
                        dve.wait_ge(x2_ok, t.n + 1)
                        apart(dve, passed)
                        stats(st2, mv2, t.n - 3, t.mod(8) // 4, ln2_stats, t.per(4))
                t = at(L_RT)
                if t.live(NT) and t.mod(4) == 3:
                    weigh(t)
            steps(dve, NT + L_SCAT + 1, PRO, NT, step)

            link = run(dve, tb_chain, 0, 0)
            nc.vector.tensor_copy(tail[0:1, :], base[0:1, SEQS, :]).then_inc(tail_ok, 1)
            link(nc.vector.tensor_tensor(cnt[:, :], base[:, 1:, :].rearrange("p g e -> p (g e)"), first_slot,
                                         ALU.subtract))
            link(nc.vector.tensor_scalar(cnt_i[:, :], cnt[:, :], float(P - 1), None, ALU.add))
            link(nc.vector.tensor_scalar(cnt_i[:, :], cnt_i[:, :], P.bit_length() - 1, None, ALU.arith_shift_right))
            link(nc.vector.tensor_copy(cb[:, :], cnt_i[:, :]))
            nc.vector.memset(start[:, 0:EXP], 0.0)
            link(nc.vector.tensor_copy(start[:, EXP:CELLS], cb[:, 0:CELLS - EXP]))
            link(nc.vector.tensor_tensor(nblk[:, :], cb[:, :], start[:, :], ALU.subtract))

            def running(a, to, unit, op):
                shift, turn = unit, 0
                while shift < CELLS:
                    b = to[turn % 2]
                    nc.vector.tensor_copy(b[:, 0:shift], a[:, 0:shift])
                    link(nc.vector.tensor_tensor(b[:, shift:CELLS], a[:, shift:CELLS], a[:, 0:CELLS - shift], op))
                    a, shift, turn = b, 2 * shift, turn + 1
                return a
            ends = running(nblk, cum, 1, ALU.add)
            link(nc.vector.tensor_tensor(cnt[:, :], cb[:, :], ends[:, :], ALU.subtract))
            nc.vector.tensor_scalar(off[:, CELLS:CELLS + 1], ends[:, CELLS - 1:CELLS], -float(P), float(EXP * CAP),
                                    ALU.mult, ALU.add)
            link(nc.vector.scalar_tensor_tensor(out=off[:, 0:CELLS], in0=cnt[:, :], scalar=float(P), in1=first_slot,
                                                op0=ALU.mult, op1=ALU.add))
            link(nc.vector.tensor_tensor(delta[:, :], off[:, 1:CELLS + 1], off[:, 0:CELLS], ALU.subtract))
            for n in range(2):
                for k, d in enumerate((delta[:, :], step_expert)):
                    last = nc.vector.scalar_tensor_tensor(out=ind[:, 2 * k + n, :], in0=ends[:, :],
                                                          scalar=block_no[:, n:n + 1], in1=d,
                                                          op0=ALU.is_le, op1=ALU.mult)
            link(last)
            link(nc.vector.tensor_reduce(cols[:, :], ind[:, :, :], AX.X, ALU.add))
            nc.vector.scalar_tensor_tensor(out=cols[:, 0:2], in0=block_no, scalar=float(P), in1=cols[:, 0:2],
                                           op0=ALU.mult, op1=ALU.add).then_inc(cols_ok, 1)
            link(nc.vector.scalar_tensor_tensor(out=start[:, :], in0=start[:, :], scalar=float(P), in1=first_slot,
                                                op0=ALU.mult, op1=ALU.add))
            nc.vector.memset(low[0][:, 0:EXP], 0.0)
            link(nc.vector.scalar_tensor_tensor(out=low[0][:, EXP:CELLS], in0=nblk[:, 0:CELLS - EXP], scalar=0.0,
                                                in1=cnt[:, 0:CELLS - EXP], op0=ALU.is_gt, op1=ALU.mult))
            least = running(low[0], (low[1], low[0]), EXP, ALU.min)
            dve.wait_ge(colsT_done, 1)
            nc.vector.tensor_copy(tabs_flat[0:1, :], pm[0:1, :]).then_inc(tabs_ok, 1)
            limits_v, shifts_v = (a[:, :, :].rearrange("p g (e n) -> p (g e) n", n=2) for a in (limits, shifts))
            nc.vector.tensor_copy(limits_v[:, :, 0], first_slot)
            nc.vector.tensor_copy(limits_v[:, :, 1], start[:, :])
            nc.vector.scalar_tensor_tensor(out=shifts_v[:, :, 0], in0=least[:, :], scalar=float(P), in1=first_slot,
                                           op0=ALU.mult, op1=ALU.add)
            link(nc.vector.tensor_copy(shifts_v[:, :, 1], off[:, 0:CELLS]))
            wide = [P, SEQS, 2 * TPS, 2 * EXP]
            nc.vector.tensor_tensor(past[:, :, :, :], slot_all[:, :, :].unsqueeze(3).to_broadcast(wide),
                                    limits[:, :, :].unsqueeze(2).to_broadcast(wide), ALU.is_ge)
            nc.vector.tensor_copy(jumps[:, :, 0], shifts[:, :, 0])
            nc.vector.tensor_tensor(jumps[:, :, 1:], shifts[:, :, 1:], shifts[:, :, 0:2 * EXP - 1], ALU.subtract)\
              .then_inc(limits_ok, 1)

            def slot(at):
                b = at(B_GU)
                if b.live(NB):
                    dve.wait_ge(sil_ok, b.n + 1)
                    wait(dve, ht_done, b.n - 3)
                    nc.vector.tensor_tensor(h[:, b.mod(4), :], sil[:, b.mod(2), :], chb[:, b.mod(2), FF:2 * FF],
                                            ALU.mult).then_inc(h_ok, 1)
                b = at(B_DN)
                if b.live(NB):
                    dve.wait_ge(dn_done, b.n + 1)
                    wait(dve, yb_out[b.mod(4)], b.per(4) * 16)
                    nc.vector.tensor_copy(yb[:, b.mod(4), :], dn_ps[b.mod(2)][:, 0:DIM]).then_inc(yb_ok, 1)

            def combine(m, r):
                k = m * 8 + r
                dve.wait_ge(gath[r], (m + 1) * 32)
                wait(dve, comb_ok, k - 1)
                nc.vector.scalar_tensor_tensor(out=acc[:, r % 2, :], in0=ga[:, r, 0, :], scalar=w12[:, k, 0:1],
                                               in1=xa[:, k, :], op0=ALU.mult, op1=ALU.add).then_inc(acc_ok, 1)
                dve.wait_ge(acc_ok, k + 1)
                wait(dve, stored[r % 4 // 2], (m * 2 + r // 4) * 16)
                nc.vector.scalar_tensor_tensor(out=oo[:, r % 4, :], in0=ga[:, r, 1, :], scalar=w12[:, k, 1:2],
                                               in1=acc[:, r % 2, :], op0=ALU.mult, op1=ALU.add).then_inc(comb_ok, 1)

            def turn(i, m=None, half=0):
                for u in range(U):
                    slot(lambda lag, u=u: At(i, u - lag))
                    if m is not None and u % 2:
                        combine(m, half * TPS + u // 2)

            turn(0)
            with dve.Fori(1, C_FIRST) as i:
                turn(i)
            turn(C_FIRST, 0, 0)
            turn(C_FIRST + 1, 0, 1)
            in_b = (NB // U - C_FIRST) // 2
            with dve.Fori(1, in_b) as m:
                for half in range(2):
                    turn(m * 2 + C_FIRST + half, m, half)
            turn(NB // U - 1, in_b, 0)
            for s in range(NB, NB + B_STORE):
                slot(lambda lag, s=s: At(s // U, s % U - lag))
            for r in range(TPS, 2 * TPS):
                combine(in_b, r)
            with dve.Fori(in_b + 1, NT // 8) as m:
                for r in range(2 * TPS):
                    combine(m, r)

        @block.gpsimd
        def _(pool):
            def step(at):
                t = at(L_KBD)
                if t.live(NT):
                    pool.wait_ge(kprev_ok, t.n + 1)
                    wait(pool, smax_done, t.n - 3)
                    nc.gpsimd.tensor_tensor(
                        kbdr[:, t.mod(4), :, :, :],
                        qk[:, t.mod(4), QF:QF + 2 * KF].rearrange("p (h k) -> p h k", h=2).unsqueeze(2)
                        .to_broadcast([P, 2, KV, WIN]),
                        kvmask[:, :, :].unsqueeze(1).to_broadcast([P, 2, KV, WIN]), ALU.mult).then_inc(kbdr_ok, 1)
                t = at(L_RMS)
                if t.live(NT):
                    r = t.mod(4)
                    pool.wait_ge(t12_ok, t.n + 1)
                    nc.gpsimd.tensor_tensor(t3[:, r, :], t1[:, r, :], t2[:, r, :], ALU.add).then_inc(t3_ok, 1)
                    pool.wait_ge(t3_ok, t.n + 1)
                    pool.wait_ge(rms_ok, t.n + 1)
                    wait(pool, tr_ok, t.n - 3)
                    nc.gpsimd.tensor_tensor(t4[:, r, :].rearrange("p (h d) -> p h d", d=HD),
                                            t3[:, r, :].rearrange("p (h d) -> p h d", d=HD),
                                            rr[:, r, :].unsqueeze(2).to_broadcast([P, RF // HD, HD]), ALU.mult)\
                      .then_inc(t4_ok, 1)
                t = at(L_SCAT)
                if t.live(NT):
                    par = t.mod(8) // 4
                    pool.wait_ge(slot_ok, t.per(4) + 1)
                    apart(pool, passed)
                    for k in range(2):
                        nc.gpsimd.indirect_dma_start(
                            xs_dram, bass.IndirectOffsetOnAxis(ap=slot_r[:, par, k, t.mod(4):t.mod(4) + 1], axis=0),
                            xn2[:, t.mod(8), :], None).then_inc(scat[par], 16)

            pool.wait_ge(c_mem, 1)
            pool.wait_ge(c_attn, 20 * 16)
            steps(pool, NT + L_SCAT + 1, PRO, NT, step)

            pool.wait_ge(limits_ok, 1)
            wide = [P, SEQS, 2 * TPS, 2 * EXP]
            link = run(pool, row_chain, 0, 0)
            link(nc.gpsimd.tensor_tensor(past[:, :, :, :], past[:, :, :, :],
                                         jumps[:, :, :].unsqueeze(2).to_broadcast(wide), ALU.mult))
            half = EXP
            while half:
                link(nc.gpsimd.tensor_tensor(past[:, :, :, 0:half], past[:, :, :, 0:half],
                                             past[:, :, :, half:2 * half], ALU.add))
                half //= 2
            link(nc.gpsimd.tensor_tensor(slot_all[:, :, :], slot_all[:, :, :], past[:, :, :, 0], ALU.subtract))
            link(nc.gpsimd.tensor_copy(row_all[:, :, :].rearrange("p (q v) k -> p q (v k)", q=SEQS),
                                       slot_all[:, :, :]))
            for q in range(SEQS):
                blocks = 2 * TPS * (q + 1) + SLACK + 1
                for n in range(4):
                    pool.wait_ge(yb_out[n], blocks // 4 * 16)
                wait(pool, comb_ok, (q - 1) * TPS)
                for v in range(TPS):
                    for j in range(2):
                        nc.gpsimd.indirect_dma_start(
                            ga[:, q % 2 * TPS + v, j, :], None, ys_dram[0:blocks * P, :],
                            bass.IndirectOffsetOnAxis(ap=row_all[:, q * TPS + v, j:j + 1], axis=0))\
                          .then_inc(gath[q % 2 * TPS + v], 16)

    return nc


def _layouts(a):
    heads = [g * J + j for j in range(J) for g in range(KV)]
    qrow = np.array([h * HD + d for h in heads for d in range(HD)])
    swap = np.array([(d + HD // 2) % HD for d in range(HD)])
    qswap = np.array([h * HD + d for h in heads for d in swap])
    kswap = np.array([g * HD + d for g in range(KV) for d in swap])
    partner = np.array([(h ^ 1) * HD + d for h in heads for d in range(HD)])
    wq, wk, wv, wo = (a["L0_attn_" + n] for n in ("Wq", "Wk", "Wv", "Wo"))
    mix = a["L0_attn_pair_mix"]
    hq = np.repeat(np.array(heads), HD)
    return {
        "x": a["L0_attn_x"].reshape(TOK, DIM),
        "w_proj": np.concatenate([wq[qrow], wk, wq[qswap], wk[kswap], wv]).T,
        "gain": np.broadcast_to(a["L0_attn_q_gain"][hq], (P, QF)),
        "wo_self": wo.T[qrow], "wo_pair": wo.T[partner],
        "mix_self": mix[hq // 2, hq % 2, hq % 2][:, None],
        "mix_pair": mix[hq // 2, 1 - hq % 2, hq % 2][:, None],
        "w_router": a["L0_ffn_router_w"].T,
        "w_gu": np.concatenate([a["L0_ffn_w_gate"], a["L0_ffn_w_up"]], axis=1).transpose(2, 0, 1),
        "w_dn": a["L0_ffn_w_down"].reshape(EXP, DIM, 2, P).transpose(3, 0, 2, 1),
    }


def _constants():
    bfloat16 = mybir.dt.np(BF16)
    f = np.float32
    inv = (1.0 / f(10000.0) ** (np.arange(0, HD, 2, dtype=f) / f(HD))).astype(f)
    ang = np.outer(np.arange(SEQ, dtype=f), inv).astype(f)
    cos = np.concatenate([np.cos(ang), np.cos(ang)], 1)
    sin = np.concatenate([np.sin(ang), -np.sin(ang)], 1)
    rope = np.stack([np.concatenate([np.tile(m, (1, HEADS)), np.tile(m, (1, KV)) * HD ** 0.5], 1)
                     for m in (cos, sin)], 1).astype(f)
    own = np.arange(KF) // HD
    kv = (own[:, None] == np.arange(KV)[None, :]).astype(f)
    q, k = np.arange(WIN)[:, None], np.arange(WIN)[None, :]
    cur, old = np.where(k <= q, 0, NEG), np.where(k > q, 0, NEG)
    smq, smk = np.zeros((P, P)), np.zeros((P, 2 * P))
    smq[:WIN] = np.tile(np.eye(WIN), (1, J))
    smk[:WIN] = np.concatenate([np.tile(cur, (1, KV)), np.tile(old, (1, KV))], 1)
    stsel = np.zeros((P, CH, KV, WIN))
    for c in range(CH):
        for g in range(KV):
            stsel[c * KV + g, c, g] = stsel[CH * KV + c * KV + g, c, g] = 1
    stsel[2 * CH * KV:2 * CH * KV + WIN] = np.tile(np.eye(WIN)[:, None, None, :], (1, CH, KV, 1))
    stmask = np.zeros((P - 2 * CH * KV, 2, P))
    stmask[:WIN] = np.stack([np.tile(cur.T, (1, J)), np.tile(old.T, (1, J))], 1)
    cell_e = np.tile(np.arange(EXP), SEQS)
    step_e = np.append(cell_e[1:] - cell_e[:-1], 0)
    cells = np.concatenate([np.broadcast_to(cell_e * CAP, (P, CELLS)), np.broadcast_to(step_e, (P, CELLS)),
                            np.arange(P)[:, None], P + np.arange(P)[:, None],
                            np.broadcast_to(EXP - np.arange(EXP), (P, EXP))], 1)
    return {
        "rope": rope.reshape(TPS, P, 2, RF).transpose(1, 0, 2, 3),
        "ident_in": np.eye(P, dtype=f), "ident16_in": np.eye(P).astype(bfloat16),
        "kvmask_in": np.broadcast_to(np.tile(kv, (CH, 1))[:, :, None], (P, KV, WIN)).astype(f),
        "oneblk_in": np.repeat(np.repeat(np.eye(KV), WIN, 0), HD, 1).astype(f),
        "smq_in": smq.astype(bfloat16), "smk_in": smk.astype(bfloat16),
        "stsel_in": stsel.reshape(P, CH, P).astype(bfloat16),
        "stmask_in": stmask.astype(bfloat16),
        "tri_in": np.stack([np.triu(np.ones((P, P)), 1), np.ones((P, P))], 1).astype(bfloat16),
        "region_in": np.broadcast_to(np.arange(EXP) * CAP, (P, EXP)).astype(f),
        "cells_in": cells.astype(f),
    }


def kernel(**inputs):
    import concourse.bacc as bacc
    from concourse.bass_utils import run_bass_kernel_spmd

    nc = bacc.Bacc("TRN2", target_bir_lowering=False, num_devices=1)
    given = _layouts({k: np.asarray(v) for k, v in inputs.items()})
    given.update(_constants())
    arrays, args = {}, {}
    for name, a in given.items():
        a = np.ascontiguousarray(a)
        arrays[name] = a
        args[name] = nc.dram_tensor(name, a.shape, mybir.dt.from_np(a.dtype), kind="ExternalInput").ap()
    out = nc.dram_tensor("out", (TOK, DIM), F32, kind="ExternalOutput").ap()
    kernel_body(nc, out=out, **args)
    r = run_bass_kernel_spmd(nc, [arrays], core_ids=[0])
    return r.results[0]["out"].reshape(SEQS, SEQ, DIM)
```

```python
from contextlib import ExitStack

import concourse.bass as bass
import numpy as np
from concourse import mybir

F32 = mybir.dt.float32
F32R = mybir.dt.float32r
BF16 = mybir.dt.bfloat16
I32 = mybir.dt.int32
U32 = mybir.dt.uint32
ALU = mybir.AluOpType
ACT = mybir.ActivationFunctionType
AX = mybir.AxisListType

P = 128
SEQS, SEQ = 16, 512
DIM, HEADS, KV, HD = 128, 16, 4, 8
J = HEADS // KV
WIN = 32
CH = P // WIN
TPS = SEQ // P
NT = SEQS * TPS
TOK = SEQS * SEQ
QF, KF = HEADS * HD, KV * HD
RF = QF + KF
PF = 2 * RF + KF
EXP, FF = 8, 256
CAP = TOK + P
SLACK = EXP * (P - 1) // P
NB = 2 * NT + SLACK + 1
JITTER = 2.0 * 0.01
RT_OPS = 17
SPARE = 8
ROWS = EXP * CAP + SPARE * P
CELLS = SEQS * EXP
U = 8
RMS_EPS, LN_EPS = 1e-6, 1e-5
NEG = -1.7e38
assert NB % U == 0 and KF == WIN and QF == P

(L_XHAT, L_PROJ, L_RMS, L_TR, L_KBD, L_SMAX, L_ST, L_PV, L_OUT) = (3, 4, 5, 6, 7, 8, 9, 10, 11)
(L_WO, L_NB2, L_XN2, L_TX2, L_RT, L_RANK, L_SCAT) = (12, 13, 14, 15, 16, 18, 21)
PRO = 24
(B_LOAD, B_BT, B_GU, B_HT, B_DN, B_STORE) = (0, 2, 4, 5, 6, 7)
C_FIRST = 4


class At:

    def __init__(self, i, c):
        self.i, self.c = i, c

    def live(self, n):
        return not isinstance(self.i, int) or 0 <= U * self.i + self.c < n

    @property
    def n(self):
        return self.i * U + self.c

    def mod(self, m):
        return self.c % m

    def per(self, m):
        return self.i * (U // m) + self.c // m


def wait(eng, sem, value):
    if not isinstance(value, int) or value > 0:
        eng.wait_ge(sem, value)


def apart(eng, passed):
    eng.sem_inc(passed, 1)


def run(eng, chain, per, q, at=0):
    count = [at]

    def link(ins):
        count[0] += 1
        ins.then_inc(chain, 1)
        eng.wait_ge(chain, q * per + count[0])
    return link


def steps(eng, total, pro, end, body):
    for s in range(pro):
        body(lambda lag, s=s: At(s // U, s % U - lag))
    with eng.Fori(pro // U, end // U) as i:
        for u in range(U):
            body(lambda lag, u=u: At(i, u - lag))
    for s in range(end, total):
        body(lambda lag, s=s: At(s // U, s % U - lag))


def kernel_body(nc, x, w_proj, rope, gain, wo_self, wo_pair, mix_self, mix_pair, w_router,
                w_gu, w_dn, ident_in, ident16_in, kvmask_in, oneblk_in, smq_in, smk_in, stsel_in,
                stmask_in, tri_in, region_in, cells_in, out):
    xs_dram = nc.dram_tensor("expert_in", (ROWS, DIM), F32, kind="Internal").ap()
    ys_dram = nc.dram_tensor("expert_out", (NB * P, DIM), F32, kind="Internal").ap()
    v_dram = nc.dram_tensor("v_rows", (TOK, KF), F32, kind="Internal").ap()
    x_v = x.rearrange("(t p) d -> p t d", p=P)
    out_v = out.rearrange("(t p) d -> p t d", p=P)

    with ExitStack() as ctx:
        def sb(name, shape, dt=F32):
            return ctx.enter_context(nc.sbuf_tensor(name, shape, dt))

        def sem(name):
            return ctx.enter_context(nc.semaphore(name))

        wp = sb("wp", [P, PF])
        tab = sb("tab", [P, TPS, 2, RF])
        gn = sb("gn", [P, QF])
        wos, wop = sb("wos", [P, DIM]), sb("wop", [P, DIM])
        mixs, mixp = sb("mixs", [P, 1]), sb("mixp", [P, 1])
        wor, wo = sb("wor", [P, DIM]), sb("wo", [P, DIM])
        wr = sb("wr", [P, EXP])
        wgu = sb("wgu", [P, EXP, 2 * FF])
        wdn = sb("wdn", [P, EXP, 2, DIM])
        ident, ident16 = sb("ident", [P, P]), sb("ident16", [P, P], BF16)
        kvmask = sb("kvmask", [P, 2, KV, WIN])
        oneblk = sb("oneblk", [P, KF])
        smq, smk = sb("smq", [P, P], BF16), sb("smk", [P, 2 * P], BF16)
        stsel = sb("stsel", [P, CH, P], BF16)
        stmov = sb("stmov", [P, 2, 2, P], BF16)
        tri = sb("tri", [P, 2, P], BF16)
        region = sb("region", [P, EXP])
        cells = sb("cells", [P, 2 * CELLS + 2 + EXP + NB])
        zero = sb("zero", [P, DIM])

        xa = sb("xa", [P, NT, DIM])
        st1, mv1 = sb("st1", [P, TPS, 6]), sb("mv1", [P, 2, TPS, 2])
        ln1, rs1, nb1 = sb("ln1", [P, 2, TPS]), sb("rs1", [P, 2, TPS]), sb("nb1", [P, 2, TPS])
        st2, mv2 = sb("st2", [P, TPS, 6]), sb("mv2", [P, 2, TPS, 2])
        ln2, rs2, nb2 = sb("ln2", [P, 2, TPS]), sb("rs2", [P, 2, TPS]), sb("nb2", [P, 2, TPS])
        xh, xhT = sb("xh", [P, 4, DIM]), sb("xhT", [P, 4, P])
        sq, ss = sb("sq", [P, 4, RF]), sb("ss", [P, 4, RF // HD])
        lnr, rr = sb("lnr", [P, 4, RF // HD]), sb("rr", [P, 4, RF // HD])
        t1, t2, t3, t4 = (sb(f"t{n}", [P, 4, RF]) for n in range(1, 5))
        vtok, vext = sb("vtok", [P, 8, KF]), sb("vext", [P, 8, CH, KF])
        qk = sb("qk", [P, 4, QF + 2 * KF])
        kbd = sb("kbd", [P, 4, 2, 2, KV, WIN])
        kbdr, qr = sb("kbdr", [P, 4, 2, 2, KV, WIN], F32R), sb("qr", [P, 4, QF], F32R)
        mx, mm = sb("mx", [P, 2, CH * KV]), sb("mm", [P, 2, 2, CH * KV], BF16)
        pT = sb("pT", [P, 2, CH, 2 * P])
        nd, rec = sb("nd", [P, 2 * P]), sb("rec", [P, HEADS])
        y, yT = sb("y", [P, 2, QF]), sb("yT", [P, 2, P])
        xn2, xn2T = sb("xn2", [P, 8, DIM]), sb("xn2T", [P, TPS, P])
        lg, dd = sb("lg", [P, TPS, EXP]), sb("dd", [P, 2, TPS, EXP])
        ab, ff = sb("ab", [P, TPS, EXP]), sb("ff", [P, 2, TPS, EXP])
        m12, ee = sb("m12", [P, 2, TPS]), sb("ee", [P, 2, TPS, EXP])
        iw, mi = sb("iw", [P, TPS, EXP]), sb("mi", [P, TPS])
        oh, ms = sb("oh", [P, 2, 2, TPS, EXP]), sb("ms", [P, TPS, EXP])
        keep, sums = sb("keep", [P, 2, TPS, EXP]), sb("sums", [P, 2, TPS])
        both = sb("both", [P, 2, TPS, EXP], BF16)
        rk, prod, slotf = sb("rk", [P, TPS, EXP]), sb("prod", [P, 2, TPS, EXP]), sb("slotf", [P, 2, TPS])
        slot_r = sb("slot_r", [P, 2, 2, TPS], U32)
        slot_all = sb("slot_all", [P, SEQS, TPS * 2])
        w12 = sb("w12", [P, NT, 2])
        base = sb("base", [P, SEQS + 1, EXP])
        cnt, cnt_i, cb = sb("cnt", [P, CELLS]), sb("cnt_i", [P, CELLS], I32), sb("cb", [P, CELLS])
        start, nblk = sb("start", [P, CELLS]), sb("nblk", [P, CELLS])
        cum, low = ([sb(f"{name}{n}", [P, CELLS]) for n in range(2)] for name in ("cum", "low"))
        limits, shifts = sb("limits", [P, SEQS, 2 * EXP]), sb("shifts", [P, SEQS, 2 * EXP])
        jumps = sb("jumps", [P, SEQS, 2 * EXP])
        past = sb("past", [P, SEQS, 2 * TPS, 2 * EXP])
        row_all = sb("row_all", [P, NT, 2], U32)
        off, delta = sb("off", [P, CELLS + 1]), sb("delta", [P, CELLS])
        ind, cols = sb("ind", [P, 4, CELLS]), sb("cols", [P, 4])
        tabs, tail = sb("tabs", [1, 2 * P], I32), sb("tail", [1, EXP], I32)
        digits, packed = sb("digits", [1, NB // U, U]), sb("packed", [1, NB // U], I32)
        summed = sb("summed", [1, NB // U])
        xb, xbT = sb("xb", [P, 4, DIM]), sb("xbT", [P, 4, P])
        sil, h, hT = sb("sil", [P, 2, FF]), sb("h", [P, 4, FF]), sb("hT", [P, 4, FF])
        yb = sb("yb", [P, 4, DIM])
        ga = sb("ga", [P, 8, 2, DIM])
        acc, oo = sb("acc", [P, 2, DIM]), sb("oo", [P, 4, DIM])

        chb = ctx.enter_context(nc.psum_tensor("chb", [P, CH, 512], F32))
        pp, pv, tp, pm = (ctx.enter_context(nc.psum_tensor(n, [P, 512], F32))
                          for n in ("pp", "pv", "tp", "pm"))
        tp16 = tp[0:2 * CH * KV, P:P + P // 2].bitcast(BF16)
        LG, PREF, TOT = P, P + TPS * EXP, P + 2 * TPS * EXP

        c_attn, c_moe, c_mem, c_zero = (sem(n) for n in ("const_attn", "const_moe", "const_mem", "const_zero"))
        passed = sem("passed")
        x_in, v_saved, v_in = sem("x_in"), sem("v_saved"), sem("v_in")
        chain, rt_chain, rk_chain, tb_chain = (sem(n) for n in ("dve_chain", "rt_chain", "rk_chain", "tb_chain"))
        rec_ok, mh_ok, acc_ok = sem("rec_ok"), sem("mh_ok"), sem("acc_ok")
        ln1_stats, act_ln, rstd1, nb1_ok = sem("ln1_stats"), sem("act_ln"), sem("rstd1"), sem("nb1_ok")
        ln2_stats, rstd2, nb2_ok = sem("ln2_stats"), sem("rstd2"), sem("nb2_ok")
        xh_ok, tx_done, xhT_ok, proj_done = sem("xh_ok"), sem("tx_done"), sem("xhT_ok"), sem("proj_done")
        sq_ok, v_ok, t12_ok, ss_ok, rms_ok = (sem(n) for n in ("sq_ok", "v_ok", "t12_ok", "ss_ok", "rms_ok"))
        t3_ok, t4_ok, tr_ok, kprev_ok = sem("t3_ok"), sem("t4_ok"), sem("tr_ok"), sem("kprev_ok")
        kbd_ok, kbdr_ok, qr_ok, smax_done = sem("kbd_ok"), sem("kbdr_ok"), sem("qr_ok"), sem("smax_done")
        max_ok, mm_ok, tm_done, stm_ok = sem("max_ok"), sem("mm_ok"), sem("tm_done"), sem("stm_ok")
        st_done, exp_ok, pv_done, nd_ok, y_ok = (sem(n) for n in ("st_done", "exp_ok", "pv_done", "nd_ok", "y_ok"))
        ty_done, yT_ok, wo_done, x2_ok = sem("ty_done"), sem("yT_ok"), sem("wo_done"), sem("x2_ok")
        xn2_ok, tx2_done, xn2T_ok, lg_done = sem("xn2_ok"), sem("tx2_done"), sem("xn2T_ok"), sem("lg_done")
        lg_read, dd_ok, ee_ok, both_ok = sem("lg_read"), sem("dd_ok"), sem("ee_ok"), sem("both_ok")
        rank_done, rank_read, slot_ok = sem("rank_done"), sem("rank_read"), sem("slot_ok")
        scat = [sem(f"scattered{n}") for n in range(2)]
        cols_ok, colsT_done, tabs_ok, tail_ok, tail_in = (sem(n) for n in (
            "cols_ok", "colsT_done", "tabs_ok", "tail_ok", "tail_in"))
        xb_in = [sem(f"xb_in{n}") for n in range(4)]
        yb_out = [sem(f"yb_out{n}") for n in range(4)]
        bt_done, xbT_ok, gu_done, sil_ok, h_ok = (sem(n) for n in ("bt_done", "xbT_ok", "gu_done", "sil_ok", "h_ok"))
        ht_done, hT_ok, dn_done, yb_ok = sem("ht_done"), sem("hT_ok"), sem("dn_done"), sem("yb_ok")
        limits_ok, row_chain, comb_ok = sem("limits_ok"), sem("row_chain"), sem("comb_ok")
        gath = [sem(f"gathered{n}") for n in range(2 * TPS)]
        stored = [sem(f"stored{n}") for n in range(2)]

        bt_ps, dn_ps = (tp, pm), (pp, pv)

        constants = ((ident, ident_in), (wp, w_proj), (tab, rope), (gn, gain), (wos, wo_self),
                     (wop, wo_pair), (mixs, mix_self), (mixp, mix_pair), (wr, w_router),
                     (ident16, ident16_in), (kvmask, kvmask_in), (oneblk, oneblk_in),
                     (smq, smq_in), (smk, smk_in), (stsel, stsel_in), (tri, tri_in),
                     (region, region_in), (cells, cells_in))

        block = ctx.enter_context(nc.Block())

        @block.sync
        def _(sp):
            def load_x(q):
                sp.dma_start(xa[:, bass.ds(q * TPS, TPS), :],
                             x_v[:, bass.ds(q * TPS, TPS), :]).then_inc(x_in, 16)

            def values(q, par, after):
                wait(sp, v_ok, (q + 1) * TPS)
                apart(sp, passed)
                sp.dma_start(v_dram[bass.ds(q * SEQ, SEQ), :].rearrange("(t p) f -> p t f", p=P),
                             vtok[:, par * TPS:(par + 1) * TPS, :]).then_inc(v_saved, 16)
                sp.wait_ge(v_saved, (q + 1) * 16)
                apart(sp, passed)
                if after:
                    wait(sp, pv_done, (q - 1) * TPS)
                    apart(sp, passed)
                src = v_dram[bass.ds(q * SEQ, SEQ), :].rearrange("(t c k) f -> k t c f", c=CH, k=WIN)
                for g in range(KV):
                    sp.dma_start(vext[g * WIN:(g + 1) * WIN, par * TPS:(par + 1) * TPS, :, g * HD:(g + 1) * HD],
                                 src[:, :, :, g * HD:(g + 1) * HD]).then_inc(v_in, 16)

            for q in range(4):
                load_x(q)
                sp.wait_ge(x_in, (q + 1) * 16)
            sp.wait_ge(c_mem, 1)
            for n in range(SPARE):
                sp.dma_start(xs_dram[EXP * CAP + n * P:EXP * CAP + (n + 1) * P, :], zero[:, :]).then_inc(c_zero, 16)
            values(0, 0, False)
            values(1, 1, False)
            with sp.Fori(1, SEQS // 2 - 1) as i:
                for par in range(2):
                    load_x(i * 2 + par + 2)
                    values(i * 2 + par, par, True)
                    sp.wait_ge(x_in, (i * 2 + par + 3) * 16)
                    apart(sp, passed)
            for par in range(2):
                values(SEQS - 2 + par, par, True)
            sp.wait_ge(tail_ok, 1)
            for e in range(EXP):
                at = sp.value_load(tail[0:1, e:e + 1], min_val=0, max_val=EXP * CAP)
                sp.dma_start(xs_dram[bass.ds(at, P), :], zero[:, :]).then_inc(tail_in, 16)
            sp.wait_ge(tail_in, EXP * 16)
            sp.wait_ge(c_zero, SPARE * 16)
            for n in range(2):
                sp.wait_ge(scat[n], NT * 16)
            sp.wait_ge(tabs_ok, 1)

            def addr(b):
                return sp.value_load(tabs[0:1, bass.ds(b, 1)], min_val=0, max_val=ROWS - P)

            def load(b):
                at = addr(b.n)
                wait(sp, bt_done, b.n - 3)
                sp.dma_start(xb[:, b.mod(4), :], xs_dram[bass.ds(at, P), :])\
                  .then_inc(xb_in[b.mod(4)], 16)

            def store(b):
                sp.wait_ge(yb_ok, b.n + 1)
                sp.dma_start(ys_dram[bass.ds(b.n * P, P), :], yb[:, b.mod(4), :])\
                  .then_inc(yb_out[b.mod(4)], 16)

            def slot(at):
                b = at(B_LOAD)
                if b.live(NB):
                    load(b)
                b = at(B_STORE)
                if b.live(NB):
                    store(b)

            def store_out(k, par):
                sp.wait_ge(comb_ok, k + 2)
                apart(sp, passed)
                sp.dma_start(out_v[:, bass.ds(k, 2), :], oo[:, 2 * par:2 * par + 2, :])\
                  .then_inc(stored[par], 16)

            def turn(i, first=None, second=None):
                for u in range(U):
                    slot(lambda lag, u=u: At(i, u - lag))
                    if u == 2 and second is not None:
                        store_out(second * TPS + 2, 1)
                    if u == 6 and first is not None:
                        store_out(first * TPS, 0)

            turn(0)
            turn(1)
            with sp.Fori(2, C_FIRST) as i:
                turn(i)
            turn(C_FIRST, 0)
            with sp.Fori(C_FIRST + 1, NB // U) as i:
                turn(i, i - C_FIRST, i - C_FIRST - 1)
            for s in range(NB, NB + B_STORE):
                slot(lambda lag, s=s: At(s // U, s % U - lag))
            in_b = NB // U - C_FIRST
            store_out((in_b - 1) * TPS + 2, 1)
            with sp.Fori(in_b, SEQS) as m:
                for par in range(2):
                    store_out(m * TPS + 2 * par, par)
            for n in range(2):
                sp.wait_ge(stored[n], NT // 4 * 16)

        @block.scalar
        def _(act):
            for dst, src in constants:
                act.dma_start(dst[:], src).then_inc(c_attn, 16)
            for r in range(2):
                act.dma_start(stmov[2 * CH * KV:P, r, :, :], stmask_in).then_inc(c_attn, 16)
            act.dma_start(wgu[:, :, :], w_gu).then_inc(c_moe, 16)
            act.dma_start(wdn[:, :, :, :], w_dn).then_inc(c_moe, 16)
            act.preload_act_table_set("natural_log_exp_and_others")

            def step(at):
                t = at(L_PROJ)
                if t.live(NT):
                    act.wait_ge(tx_done, t.n + 1)
                    wait(act, proj_done, t.n - 3)
                    nc.scalar.copy(xhT[:, t.mod(4), :], pp[:, PF:PF + P]).then_inc(xhT_ok, 1)
                t = at(L_KBD)
                if t.live(NT):
                    r = t.mod(4)
                    act.wait_ge(tr_ok, t.n + 1)
                    if r > 0:
                        nc.scalar.copy(qk[0:WIN, r, RF:RF + KF], qk[P - WIN:P, r - 1, QF:RF])
                    for c in range(CH - 1):
                        last = nc.scalar.copy(qk[(c + 1) * WIN:(c + 2) * WIN, r, RF:RF + KF],
                                              qk[c * WIN:(c + 1) * WIN, r, QF:RF])
                    last.then_inc(kprev_ok, 1)
                t = at(L_RMS)
                if t.live(NT):
                    r = t.mod(4)
                    act.wait_ge(ss_ok, t.n + 1)
                    nc.scalar.activation(lnr[:, r, :], ss[:, r, :], ACT.Ln, bias=HD * RMS_EPS).then_inc(act_ln, 1)
                    act.wait_ge(act_ln, t.n + 1)
                    wait(act, t4_ok, t.n - 3)
                    nc.scalar.activation(rr[:, r, :], lnr[:, r, :], ACT.Exp, scale=-0.5).then_inc(rms_ok, 1)
                t = at(L_KBD)
                if t.live(NT):
                    wait(act, smax_done, 2 * t.n - 6)
                    nc.scalar.copy(qr[:, t.mod(4), :], qk[:, t.mod(4), 0:QF]).then_inc(qr_ok, 1)
                t = at(L_PROJ)
                if t.live(NT):
                    act.wait_ge(proj_done, t.n + 1)
                    wait(act, ss_ok, t.n - 3)
                    nc.scalar.activation(sq[:, t.mod(4), :], pp[:, 0:RF], ACT.Square).then_inc(sq_ok, 1)
                    if t.mod(4) == 0:
                        wait(act, v_saved, (t.per(4) - 1) * 16)
                    nc.scalar.copy(vtok[:, t.mod(8), :], pp[:, 2 * RF:PF]).then_inc(v_ok, 1)
                t = at(L_XHAT)
                if t.live(NT):
                    v, par = t.mod(4), t.mod(8) // 4
                    act.wait_ge(nb1_ok, t.per(4) + 1)
                    wait(act, tx_done, t.n - 3)
                    nc.scalar.activation(xh[:, v, :], xa[:, t.n, :], ACT.Identity, scale=rs1[:, par, v:v + 1],
                                         bias=nb1[:, par, v:v + 1]).then_inc(xh_ok, 1)
                for half in range(2):
                    t = at(L_XN2 + half)
                    if t.live(NT) and t.mod(4) == 3:
                        par = t.mod(8) // 4
                        act.wait_ge(nb2_ok, t.per(4) + 1)
                        wait(act, scat[par], t.per(8) * 2 * TPS * 16)
                        for v in (2 * half, 2 * half + 1):
                            last = nc.scalar.activation(xn2[:, TPS * par + v, :], xa[:, t.n - 3 + v, :], ACT.Identity,
                                                        scale=rs2[:, par, v:v + 1], bias=nb2[:, par, v:v + 1])
                        last.then_inc(xn2_ok, 1)
                for lag, u, stats, per, mv, ln, rs, done in (
                        (2, 0, ln1_stats, 3, mv1, ln1, rs1, rstd1),
                        (L_NB2, 3, ln2_stats, TPS + 1, mv2, ln2, rs2, rstd2)):
                    t = at(lag)
                    if t.live(NT) and t.mod(4) == u:
                        par, q = t.mod(8) // 4, t.per(4)
                        act.wait_ge(stats, per * (q + 1))
                        nc.scalar.activation(ln[:, par, :], mv[:, par, :, 1], ACT.Ln, bias=LN_EPS).then_inc(done, 1)
                        act.wait_ge(done, 2 * q + 1)
                        nc.scalar.activation(rs[:, par, :], ln[:, par, :], ACT.Exp, scale=-0.5).then_inc(done, 1)
                t = at(L_ST)
                if t.live(NT):
                    r = t.mod(2)
                    wait(act, pv_done, t.n - 1)
                    for half in range(2):
                        act.wait_ge(st_done, 2 * t.n + half + 1)
                        if t.mod(4) == 0 and half == 0:
                            nc.scalar.activation(pT[:, r, 0, 0:P], chb[:, 0, 0:P], ACT.Exp)
                            last = nc.scalar.activation(pT[:, r, 1, :], chb[:, 1, 0:2 * P], ACT.Exp)
                        else:
                            two = slice(2 * half, 2 * half + 2)
                            last = nc.scalar.activation(pT[:, r, two, :], chb[:, two, 0:2 * P], ACT.Exp)
                        last.then_inc(exp_ok, 1)
                t = at(L_SMAX)
                if t.live(NT):
                    act.wait_ge(tm_done, t.n + 1)
                    wait(act, st_done, 2 * t.n - 2)
                    nc.scalar.copy(stmov[0:2 * CH * KV, t.mod(2), :, :],
                                   tp16.unsqueeze(1).to_broadcast([2 * CH * KV, 2, P])).then_inc(stm_ok, 1)
                t = at(L_KBD)
                if t.live(NT):
                    act.wait_ge(kbd_ok, t.n + 1)
                    nc.scalar.copy(kbdr[:, t.mod(4), :, :, :, :], kbd[:, t.mod(4), :, :, :, :]).then_inc(kbdr_ok, 1)
                t = at(L_OUT)
                if t.live(NT):
                    act.wait_ge(ty_done, t.n + 1)
                    wait(act, wo_done, t.n - 1)
                    nc.scalar.copy(yT[:, t.mod(2), :], tp[:, 2 * P:3 * P]).then_inc(yT_ok, 1)
                t = at(L_RT + 1)
                if t.live(NT) and t.mod(4) == 3:
                    act.wait_ge(dd_ok, t.per(4) + 1)
                    nc.scalar.activation(ee[:, :, :, :], dd[:, :, :, :], ACT.Exp).then_inc(ee_ok, 1)
                t = at(L_TX2)
                if t.live(NT) and t.mod(4) == 3:
                    act.wait_ge(tx2_done, t.per(4) + 1)
                    wait(act, lg_done, t.per(4))
                    nc.scalar.copy(xn2T[:, :, :], tp[:, :].rearrange("p (v n) -> p v n", v=TPS)).then_inc(xn2T_ok, 1)

            act.wait_ge(c_mem, 1)
            steps(act, NT + L_SCAT + 1, PRO, NT, step)

            def slot(at):
                b = at(B_BT)
                if b.live(NB):
                    act.wait_ge(bt_done, b.n + 1)
                    wait(act, gu_done, b.n - 3)
                    nc.scalar.copy(xbT[:, b.mod(4), :], bt_ps[b.mod(2)][:, 0:P]).then_inc(xbT_ok, 1)
                b = at(B_HT)
                if b.live(NB):
                    act.wait_ge(ht_done, b.n + 1)
                    wait(act, dn_done, b.n - 3)
                    nc.scalar.copy(hT[:, b.mod(4), :], chb[:, 2 + b.mod(2), 0:FF]).then_inc(hT_ok, 1)
                b = at(B_GU)
                if b.live(NB):
                    act.wait_ge(gu_done, b.n + 1)
                    wait(act, h_ok, b.n - 1)
                    nc.scalar.activation(sil[:, b.mod(2), :], chb[:, b.mod(2), 0:FF], ACT.Silu).then_inc(sil_ok, 1)

            act.preload_act_table_set("silu_and_others")
            steps(act, NB + B_STORE, 2 * U, NB, slot)

        @block.tensor
        def _(pe):
            pe.wait_ge(c_attn, 20 * 16)
            pe.wait_ge(c_mem, 3)

            def step(at):
                t = at(L_PROJ)
                if t.live(NT):
                    pe.wait_ge(xh_ok, t.n + 1)
                    wait(pe, t12_ok, t.n)
                    nc.tensor.transpose(pp[:, PF:PF + P], xh[:, t.mod(4), :], ident[:, :]).then_inc(tx_done, 1)
                t = at(L_SMAX)
                if t.live(NT):
                    r = t.mod(4)
                    pe.wait_ge(kbdr_ok, t.n + 1)
                    pe.wait_ge(qr_ok, t.n + 1)
                    for pair in range(2):
                        wait(pe, exp_ok, 2 * t.n - 3 + pair)
                        rows = slice(pair * 2 * WIN, (pair + 1) * 2 * WIN)
                        both_chunks = [(c, P if r == 0 and c == 0 else 2 * P) for c in (2 * pair, 2 * pair + 1)]
                        for c, w in both_chunks:
                            nc.tensor.matmul(chb[:, c, 0:w], smq[:, :], smk[:, 0:w], start=True, stop=False)
                        for c, w in both_chunks:
                            k = kbdr[rows, r, c % 2, :, :, :].rearrange("p a b c -> p (a b c)")
                            last = nc.tensor.matmul(chb[:, c, 0:w], qr[rows, r, :], k[:, 0:w],
                                                    start=False, stop=True)
                        last.then_inc(smax_done, 1)
                t = at(L_RANK)
                if t.live(NT) and t.mod(4) == 3:
                    pe.wait_ge(both_ok, t.per(4) + 1)
                    b = at(L_WO + 1)
                    pe.wait_ge(x2_ok, b.n + 1 if b.live(NT) else NT)
                    pref = pm[:, PREF:PREF + TPS * EXP].rearrange("p (v e) -> p v e", v=TPS)
                    m = both[:, t.mod(8) // 4, :, :]
                    nc.tensor.matmul(pm[:, PREF:PREF + TPS * EXP], tri[:, 0, :], m.rearrange("p v e -> p (v e)"),
                                     start=True, stop=False, skip_group_check=True)
                    for v in range(TPS - 1):
                        n = TPS - 1 - v
                        nc.tensor.matmul(pref[:, v + 1:TPS, :], tri[:, 1, :],
                                         m[:, v, :].unsqueeze(1).to_broadcast([P, n, EXP]),
                                         start=False, stop=(v == TPS - 2), skip_group_check=True)
                    for v in range(TPS):
                        last = nc.tensor.matmul(pm[:, TOT:TOT + EXP], tri[:, 1, :], m[:, v, :], start=False,
                                                stop=(v == TPS - 1), skip_group_check=True)
                    last.then_inc(rank_done, 1)
                t = at(L_WO)
                if t.live(NT):
                    pe.wait_ge(yT_ok, t.n + 1)
                    b = at(L_RANK + 1)
                    if b.live(NT) and b.mod(4) == 3:
                        pe.wait_ge(rank_read, b.per(4) + 1)
                    b = at(L_RT + 1)
                    if b.live(NT) and b.mod(4) == 3:
                        pe.wait_ge(lg_read, b.per(4) + 1)
                    nc.tensor.matmul(pm[:, 0:DIM], yT[:, t.mod(2), :], wo[:, :], start=True, stop=True)\
                      .then_inc(wo_done, 1)
                t = at(L_PROJ)
                if t.live(NT):
                    pe.wait_ge(xhT_ok, t.n + 1)
                    nc.tensor.matmul(pp[:, 0:PF], xhT[:, t.mod(4), :], wp[:, :], start=True, stop=True)\
                      .then_inc(proj_done, 1)
                t = at(L_ST)
                if t.live(NT):
                    r = t.mod(4)
                    pe.wait_ge(stm_ok, t.n + 1)
                    mov = stmov[:, t.mod(2), :, :].rearrange("p a b -> p (a b)")
                    k = kbd[:, r, :, :, :, :].rearrange("p n a b c -> p n a (b c)")
                    for pair in range(2):
                        b = at(L_SMAX)
                        if b.live(NT):
                            pe.wait_ge(max_ok, 2 * b.n + pair + 1)
                        else:
                            wait(pe, exp_ok, 2 * t.n - 1 + pair)
                        rows = slice(pair * 2 * WIN, (pair + 1) * 2 * WIN)
                        both_chunks = [(c, 1 if r == 0 and c == 0 else 2) for c in (2 * pair, 2 * pair + 1)]
                        for c, halves in both_chunks:
                            nc.tensor.matmul(chb[:, c, 0:halves * P], stsel[:, c, :], mov[:, 0:halves * P],
                                             start=True, stop=False)
                        for c, halves in both_chunks:
                            for half in range(halves):
                                last = nc.tensor.matmul(chb[:, c, half * P:(half + 1) * P], k[rows, c % 2, half, :],
                                                        qk[rows, r, 0:QF], start=False, stop=(half == halves - 1))
                        last.then_inc(st_done, 1)
                t = at(L_RT)
                if t.live(NT) and t.mod(4) == 3:
                    pe.wait_ge(xn2T_ok, t.per(4) + 1)
                    b = at(L_WO)
                    if b.live(NT):
                        pe.wait_ge(x2_ok, b.n + 1)
                    b = at(L_RANK + 2)
                    if b.live(NT):
                        pe.wait_ge(rank_read, b.per(4) + 1)
                    for v in range(TPS):
                        last = nc.tensor.matmul(pm[:, LG + v * EXP:LG + (v + 1) * EXP], xn2T[:, v, :], wr[:, :],
                                                start=True, stop=True)
                    last.then_inc(lg_done, 1)
                t = at(L_SMAX)
                if t.live(NT):
                    pe.wait_ge(mm_ok, t.n + 1)
                    b = at(L_TX2 + 1)
                    if b.live(NT) and b.mod(4) == 3:
                        pe.wait_ge(xn2T_ok, b.per(4) + 1)
                    b = at(L_OUT + 1)
                    if b.live(NT):
                        pe.wait_ge(yT_ok, b.n + 1)
                    nc.tensor.transpose(tp16, mm[:, t.mod(2), :, :].rearrange("p a b -> p (a b)"), ident16[:, :])\
                      .then_inc(tm_done, 1)
                t = at(L_PV)
                if t.live(NT):
                    r = t.mod(8)
                    pe.wait_ge(exp_ok, 2 * t.n + 2)
                    pe.wait_ge(v_in, (t.per(4) + 1) * KV * 16)
                    wait(pe, nd_ok, t.n)
                    for what in range(2):
                        for half in range(2):
                            for c in range(CH):
                                first = t.mod(4) == 0 and c == 0
                                if half == 1 and first:
                                    continue
                                if what == 1:
                                    lhs = oneblk[:, :]
                                elif half == 0:
                                    lhs = vext[:, r, c, :]
                                else:
                                    lhs = vext[:, r, c - 1, :] if c else vext[:, r - 1, CH - 1, :]
                                last = nc.tensor.matmul(pv[c * WIN:(c + 1) * WIN, what * P:(what + 1) * P], lhs,
                                                        pT[:, t.mod(2), c, half * P:(half + 1) * P],
                                                        start=(half == 0), stop=(half == 1 or first),
                                                        tile_position=(0, c * WIN))
                    last.then_inc(pv_done, 1)
                t = at(L_OUT)
                if t.live(NT):
                    pe.wait_ge(y_ok, t.n + 1)
                    b = at(L_SMAX)
                    if b.live(NT):
                        pe.wait_ge(stm_ok, b.n + 1)
                    else:
                        b = at(L_TX2 + 1)
                        if b.live(NT) and b.mod(4) == 3:
                            pe.wait_ge(xn2T_ok, b.per(4) + 1)
                        wait(pe, yT_ok, t.n)
                    nc.tensor.transpose(tp[:, 2 * P:3 * P], y[:, t.mod(2), :], ident[:, :]).then_inc(ty_done, 1)
                t = at(L_TX2)
                if t.live(NT) and t.mod(4) == 3:
                    par = t.mod(8) // 4
                    pe.wait_ge(xn2_ok, 2 * (t.per(4) + 1))
                    b = at(L_SMAX)
                    if b.live(NT):
                        pe.wait_ge(stm_ok, b.n + 1)
                    b = at(L_OUT)
                    if b.live(NT):
                        pe.wait_ge(yT_ok, b.n + 1)
                    for v in range(TPS):
                        last = nc.tensor.transpose(tp[:, v * P:(v + 1) * P], xn2[:, TPS * par + v, :], ident[:, :])
                    last.then_inc(tx2_done, 1)

            steps(pe, NT + L_SCAT + 1, PRO, NT, step)

            pe.wait_ge(cols_ok, 1)
            for n in range(4):
                last = nc.tensor.transpose(pm[0:1, n * P:(n + 1) * P], cols[:, n:n + 1], ident[:, :])
            last.then_inc(colsT_done, 1)
            pe.wait_ge(tabs_ok, 1)
            pe.wait_ge(c_moe, 32)

            def experts(i):
                return pe.value_load(packed[0:1, bass.ds(i, 1)], min_val=0, max_val=EXP ** U - 1)

            def slot(at, expert, load=None):
                b = at(B_GU)
                if b.live(NB):
                    e = expert(b)
                    pe.wait_ge(xbT_ok, b.n + 1)
                    wait(pe, h_ok, b.n - 1)
                    nc.tensor.matmul(chb[:, b.mod(2), :], xbT[:, b.mod(4), :], wgu[:, e, :],
                                     start=True, stop=True).then_inc(gu_done, 1)
                if load:
                    load()
                b = at(B_DN)
                if b.live(NB):
                    e = expert(b)
                    pe.wait_ge(hT_ok, b.n + 1)
                    wait(pe, yb_ok, b.n - 1)
                    for k in range(2):
                        last = nc.tensor.matmul(dn_ps[b.mod(2)][:, 0:DIM], hT[:, b.mod(4), k * P:(k + 1) * P],
                                                wdn[:, e, k, :], start=(k == 0), stop=(k == 1))
                    last.then_inc(dn_done, 1)
                b = at(B_BT)
                if b.live(NB):
                    pe.wait_ge(xb_in[b.mod(4)], (b.per(4) + 1) * 16)
                    wait(pe, xbT_ok, b.n - 1)
                    nc.tensor.transpose(bt_ps[b.mod(2)][:, 0:P], xb[:, b.mod(4), :], ident[:, :]).then_inc(bt_done, 1)
                b = at(B_HT)
                if b.live(NB):
                    pe.wait_ge(h_ok, b.n + 1)
                    wait(pe, hT_ok, b.n - 1)
                    for k in range(2):
                        last = nc.tensor.transpose(chb[:, 2 + b.mod(2), k * P:(k + 1) * P],
                                                   h[:, b.mod(4), k * P:(k + 1) * P], ident[:, :])
                    last.then_inc(ht_done, 1)

            def turn(i, first, second, upto=U):
                words = {}
                if first:
                    words[-1] = experts(i - 1)

                def expert(b):
                    return words[b.c // U] >> b.mod(U) * (EXP - 1).bit_length() & EXP - 1

                def load():
                    words[0] = experts(i)
                for u in range(upto):
                    slot(lambda lag, u=u: At(i, u - lag), expert, load if second and u == 1 else None)

            turn(0, False, True)
            turn(1, True, True)
            with pe.Fori(2, NB // U) as i:
                turn(i, True, True)
            turn(NB // U, True, False, B_STORE)

        @block.vector
        def _(dve):
            nc.vector.memset(qk[:, :, :], 0.0).then_inc(chain, 1)
            nc.vector.memset(zero[:, :], 0.0).then_inc(chain, 1)
            dve.wait_ge(chain, 2)
            nc.vector.memset(vext[:, :, :, :], 0.0).then_inc(c_mem, 1)
            dve.wait_ge(c_attn, 20 * 16)
            for u in range(TPS):
                for n in range(2):
                    nc.vector.tensor_tensor(tab[:, u, n, 0:QF], tab[:, u, n, 0:QF], gn[:, :], ALU.mult)
            nc.vector.tensor_copy(base[:, 0, :], region[:, :])
            nc.vector.tensor_scalar(wor[:, :], wop[:, :], mixp[:, 0:1], None, ALU.mult).then_inc(c_mem, 1)
            dve.wait_ge(c_mem, 2)
            nc.vector.scalar_tensor_tensor(out=wo[:, :], in0=wos[:, :], scalar=mixs[:, 0:1], in1=wor[:, :],
                                           op0=ALU.mult, op1=ALU.add).then_inc(c_mem, 1)

            first_slot = cells[:, 0:CELLS]
            step_expert = cells[:, CELLS:2 * CELLS]
            block_no = cells[:, 2 * CELLS:2 * CELLS + 2]
            powers = cells[0:1, 2 * CELLS + 2 + EXP:]
            order = cells[:, 2 * CELLS + 2:2 * CELLS + 2 + EXP]

            def over_experts(a):
                return a.unsqueeze(2).to_broadcast([P, TPS, EXP])

            def one_hot(link, k, par):
                link(nc.vector.scalar_tensor_tensor(
                    out=iw[:, :, :], in0=dd[:, k, :, :], scalar=0.0,
                    in1=order.unsqueeze(1).to_broadcast([P, TPS, EXP]), op0=ALU.is_ge, op1=ALU.mult))
                link(nc.vector.tensor_reduce(mi[:, :], iw[:, :, :], AX.X, ALU.max))
                link(nc.vector.tensor_tensor(oh[:, par, k, :, :], iw[:, :, :], over_experts(mi[:, :]), ALU.is_equal))

            def choose(t):
                q, par = t.per(4), t.mod(8) // 4
                link = run(dve, rt_chain, RT_OPS, q)
                dve.wait_ge(lg_read, q + 1)
                link(nc.vector.scalar_tensor_tensor(out=ab[:, :, :], in0=lg[:, :, :], scalar=-1.0,
                                                    in1=lg[:, :, :], op0=ALU.mult, op1=ALU.max))
                link(nc.vector.tensor_reduce(m12[:, 0, :], lg[:, :, :], AX.X, ALU.max))
                link(nc.vector.tensor_tensor(dd[:, 0, :, :], lg[:, :, :], over_experts(m12[:, 0, :]), ALU.subtract))
                one_hot(link, 0, par)
                link(nc.vector.scalar_tensor_tensor(out=ms[:, :, :], in0=oh[:, par, 0, :, :], scalar=NEG,
                                                    in1=lg[:, :, :], op0=ALU.mult, op1=ALU.add))
                link(nc.vector.tensor_reduce(m12[:, 1, :], ms[:, :, :], AX.X, ALU.max))
                wait(dve, ee_ok, q)
                nc.vector.tensor_tensor(dd[:, 1, :, :], ms[:, :, :], over_experts(m12[:, 1, :]), ALU.subtract)\
                  .then_inc(dd_ok, 1)
                dve.wait_ge(dd_ok, q + 1)

            def choose_more(t):
                q, par = t.per(4), t.mod(8) // 4
                link = run(dve, rt_chain, RT_OPS, q, 8)
                one_hot(link, 1, par)
                wait(dve, rank_done, q)
                nc.vector.tensor_tensor(both[:, par, :, :], oh[:, par, 0, :, :], oh[:, par, 1, :, :], ALU.add)\
                  .then_inc(both_ok, 1)
                for k in range(2):
                    link(nc.vector.tensor_tensor(ff[:, k, :, :], ab[:, :, :], over_experts(m12[:, k, :]), ALU.max))
                link(nc.vector.scalar_tensor_tensor(out=ff[:, :, :, :], in0=ff[:, :, :, :], scalar=JITTER,
                                                    in1=dd[:, :, :, :], op0=ALU.mult, op1=ALU.add))

            def weigh(t):
                q, par = t.per(4), t.mod(8) // 4
                link = run(dve, rt_chain, RT_OPS, q, RT_OPS - 3)
                dve.wait_ge(ee_ok, q + 1)
                link(nc.vector.scalar_tensor_tensor(out=keep[:, :, :, :], in0=ff[:, :, :, :], scalar=0.0,
                                                    in1=ee[:, :, :, :], op0=ALU.is_ge, op1=ALU.mult))
                link(nc.vector.tensor_reduce(sums[:, :, :], keep[:, :, :, :], AX.X, ALU.add))
                link(nc.vector.reciprocal(w12[:, bass.ds(t.n - 3, TPS), :].rearrange("p v k -> p k v"), sums[:, :, :]))

            def ranks(t):
                q = t.per(4)
                dve.wait_ge(rank_done, q + 1)
                wait(dve, rk_chain, 3 * q)
                nc.vector.tensor_tensor(base[:, q + 1, :], base[:, q, :], pm[:, TOT:TOT + EXP], ALU.add)
                nc.vector.tensor_tensor(rk[:, :, :], pm[:, PREF:PREF + TPS * EXP].rearrange("p (v e) -> p v e", v=TPS),
                                        base[:, q, :].unsqueeze(1).to_broadcast([P, TPS, EXP]), ALU.add)\
                  .then_inc(rank_read, 1)

            def slots(t):
                q, par = t.per(4), t.mod(8) // 4
                link = run(dve, rk_chain, 3, q)
                dve.wait_ge(rank_read, q + 1)
                link(nc.vector.tensor_tensor(prod[:, :, :, :], oh[:, par, :, :, :],
                                             rk[:, :, :].unsqueeze(1).to_broadcast([P, 2, TPS, EXP]), ALU.mult))
                link(nc.vector.tensor_reduce(slotf[:, :, :], prod[:, :, :, :], AX.X, ALU.add))
                link(nc.vector.tensor_copy(slot_all[:, q, :].rearrange("p (v k) -> p k v", k=2), slotf[:, :, :]))
                nc.vector.tensor_copy(slot_r[:, par, :, :], slotf[:, :, :]).then_inc(slot_ok, 1)

            def step(at):
                for lag, u, mv, rs, nb, ready, done in ((3, 0, mv1, rs1, nb1, rstd1, nb1_ok),
                                                        (L_NB2 + 1, 3, mv2, rs2, nb2, rstd2, nb2_ok)):
                    t = at(lag)
                    if t.live(NT) and t.mod(4) == u:
                        par = t.mod(8) // 4
                        dve.wait_ge(ready, 2 * (t.per(4) + 1))
                        nc.vector.scalar_tensor_tensor(out=nb[:, par, :], in0=mv[:, par, :, 0], scalar=-1.0,
                                                       in1=rs[:, par, :], op0=ALU.mult, op1=ALU.mult).then_inc(done, 1)
                t = at(L_SMAX)
                if t.live(NT):
                    r = t.mod(2)

                    def chunk_max(c0, c1, halves):
                        src = chb[:, c0:c1, 0:halves * P].rearrange("p c (h g k) -> p c g h k", h=halves, g=KV)
                        dst = mx[:, r, c0 * KV:c1 * KV].rearrange("p (c g) -> p c g", g=KV)
                        return nc.vector.tensor_reduce(dst, src, AX.XY, ALU.max)

                    dve.wait_ge(smax_done, 2 * t.n + 1)
                    if t.mod(4) == 0:
                        chunk_max(0, 1, 1)
                        chunk_max(1, 2, 2).then_inc(max_ok, 1)
                    else:
                        chunk_max(0, 2, 2).then_inc(max_ok, 1)
                    dve.wait_ge(smax_done, 2 * t.n + 2)
                    chunk_max(2, 4, 2).then_inc(max_ok, 1)
                t = at(L_WO)
                if t.live(NT):
                    dve.wait_ge(wo_done, t.n + 1)
                    nc.vector.tensor_tensor(xa[:, t.n, :], xa[:, t.n, :], pm[:, 0:DIM], ALU.add).then_inc(x2_ok, 1)
                t = at(L_RANK)
                if t.live(NT) and t.mod(4) == 3:
                    ranks(t)
                t = at(L_SMAX)
                if t.live(NT):
                    dve.wait_ge(max_ok, 2 * t.n + 2)
                    wait(dve, tm_done, t.n - 1)
                    nc.vector.tensor_scalar(mm[:, t.mod(2), 0, :], mx[:, t.mod(2), :], -1.0, None, ALU.mult)\
                      .then_inc(mh_ok, 1)
                t = at(L_OUT)
                if t.live(NT):
                    dve.wait_ge(pv_done, t.n + 1)
                    nc.vector.transpose(nd[:, :], pv[:, 0:2 * P]).then_inc(nd_ok, 1)
                t = at(L_SMAX)
                if t.live(NT):
                    dve.wait_ge(mh_ok, t.n + 1)
                    nc.vector.scalar_tensor_tensor(out=mm[:, t.mod(2), 1, :], in0=mx[:, t.mod(2), :], scalar=-1.0,
                                                   in1=mm[:, t.mod(2), 0, :], op0=ALU.mult, op1=ALU.subtract)\
                      .then_inc(mm_ok, 1)
                t = at(L_OUT)
                if t.live(NT):
                    dve.wait_ge(nd_ok, t.n + 1)
                    nc.vector.reciprocal(rec[:, :], nd[:, P:2 * P].rearrange("p (h d) -> p h d", d=HD)[:, :, 0])\
                      .then_inc(rec_ok, 1)
                t = at(L_TR)
                if t.live(NT):
                    dve.wait_ge(t4_ok, t.n + 1)
                    wait(dve, st_done, 2 * t.n - 6)
                    wait(dve, kprev_ok, t.n - 2)
                    nc.vector.transpose(qk[:, t.mod(4), 0:RF], t4[:, t.mod(4), :]).then_inc(tr_ok, 1)
                t = at(L_OUT)
                if t.live(NT):
                    dve.wait_ge(rec_ok, t.n + 1)
                    wait(dve, ty_done, t.n - 1)
                    nc.vector.tensor_tensor(y[:, t.mod(2), :].rearrange("p (h d) -> p h d", d=HD),
                                            nd[:, 0:P].rearrange("p (h d) -> p h d", d=HD),
                                            rec[:, :].unsqueeze(2).to_broadcast([P, HEADS, HD]), ALU.mult)\
                      .then_inc(y_ok, 1)
                t = at(L_PROJ)
                if t.live(NT):
                    r = t.mod(4)
                    dve.wait_ge(v_ok, t.n + 1)
                    wait(dve, t3_ok, t.n - 3)
                    nc.vector.tensor_tensor(t1[:, r, :], pp[:, 0:RF], tab[:, r, 0, :], ALU.mult)
                    nc.vector.tensor_tensor(t2[:, r, :], pp[:, RF:2 * RF], tab[:, r, 1, :], ALU.mult)\
                      .then_inc(t12_ok, 1)
                    dve.wait_ge(sq_ok, t.n + 1)
                    wait(dve, rms_ok, t.n - 3)
                    nc.vector.tensor_reduce(ss[:, r, :], sq[:, r, :].rearrange("p (h d) -> p h d", d=HD),
                                            AX.X, ALU.add).then_inc(ss_ok, 1)
                t = at(L_RT)
                if t.live(NT) and t.mod(4) == 3:
                    dve.wait_ge(lg_done, t.per(4) + 1)
                    wait(dve, rt_chain, t.per(4) * RT_OPS)
                    nc.vector.tensor_copy(lg[:, :, :].rearrange("p v e -> p (v e)"), pm[:, LG:LG + TPS * EXP])\
                      .then_inc(lg_read, 1)
                t = at(L_WO)
                if t.live(NT):
                    q, v = t.per(4), t.mod(4)
                    wait(dve, ln2_stats, q * (TPS + 1))
                    dve.wait_ge(x2_ok, t.n + 1)
                    apart(dve, passed)
                    nc.vector.bn_stats(st2[:, v, :], xa[:, t.n, :]).then_inc(ln2_stats, 1)
                    if v == 3:
                        dve.wait_ge(ln2_stats, (TPS + 1) * q + TPS)
                        apart(dve, passed)
                        for n in range(TPS):
                            last = nc.vector.bn_aggr(mv2[:, t.mod(8) // 4, n, :], st2[:, n, :])
                        last.then_inc(ln2_stats, 1)
                t = at(L_RT)
                if t.live(NT) and t.mod(4) == 3:
                    choose(t)
                t = at(L_RT + 1)
                if t.live(NT) and t.mod(4) == 3:
                    choose_more(t)
                t = at(L_RANK)
                if t.live(NT) and t.mod(4) == 3:
                    slots(t)
                for half in range(2):
                    t = at(half)
                    if t.live(NT) and t.mod(4) == 0:
                        dve.wait_ge(x_in, (t.per(4) + 1) * 16)
                        for v in (2 * half, 2 * half + 1):
                            last = nc.vector.bn_stats(st1[:, v, :], xa[:, t.n + v, :])
                        last.then_inc(ln1_stats, 1)
                        if half:
                            dve.wait_ge(ln1_stats, 3 * t.per(4) + 2)
                            apart(dve, passed)
                            for v in range(TPS):
                                last = nc.vector.bn_aggr(mv1[:, t.mod(8) // 4, v, :], st1[:, v, :])
                            last.then_inc(ln1_stats, 1)
                t = at(L_RT + 3)
                if t.live(NT) and t.mod(4) == 3:
                    weigh(t)
            steps(dve, NT + L_SCAT + 1, PRO, NT, step)

            link = run(dve, tb_chain, 0, 0)
            nc.vector.tensor_copy(tail[0:1, :], base[0:1, SEQS, :]).then_inc(tail_ok, 1)
            link(nc.vector.tensor_tensor(cnt[:, :], base[:, 1:, :].rearrange("p g e -> p (g e)"), first_slot,
                                         ALU.subtract))
            link(nc.vector.tensor_scalar(cnt_i[:, :], cnt[:, :], float(P - 1), None, ALU.add))
            link(nc.vector.tensor_scalar(cnt_i[:, :], cnt_i[:, :], P.bit_length() - 1, None, ALU.arith_shift_right))
            link(nc.vector.tensor_copy(cb[:, :], cnt_i[:, :]))
            nc.vector.memset(start[:, 0:EXP], 0.0)
            link(nc.vector.tensor_copy(start[:, EXP:CELLS], cb[:, 0:CELLS - EXP]))
            link(nc.vector.tensor_tensor(nblk[:, :], cb[:, :], start[:, :], ALU.subtract))

            def running(a, to, unit, op):
                shift, turn = unit, 0
                while shift < CELLS:
                    b = to[turn % 2]
                    nc.vector.tensor_copy(b[:, 0:shift], a[:, 0:shift])
                    link(nc.vector.tensor_tensor(b[:, shift:CELLS], a[:, shift:CELLS], a[:, 0:CELLS - shift], op))
                    a, shift, turn = b, 2 * shift, turn + 1
                return a
            ends = running(nblk, cum, 1, ALU.add)
            link(nc.vector.tensor_tensor(cnt[:, :], cb[:, :], ends[:, :], ALU.subtract))
            nc.vector.tensor_scalar(off[:, CELLS:CELLS + 1], ends[:, CELLS - 1:CELLS], -float(P), float(EXP * CAP),
                                    ALU.mult, ALU.add)
            link(nc.vector.scalar_tensor_tensor(out=off[:, 0:CELLS], in0=cnt[:, :], scalar=float(P), in1=first_slot,
                                                op0=ALU.mult, op1=ALU.add))
            link(nc.vector.tensor_tensor(delta[:, :], off[:, 1:CELLS + 1], off[:, 0:CELLS], ALU.subtract))
            for n in range(2):
                for k, d in enumerate((delta[:, :], step_expert)):
                    last = nc.vector.scalar_tensor_tensor(out=ind[:, 2 * k + n, :], in0=ends[:, :],
                                                          scalar=block_no[:, n:n + 1], in1=d,
                                                          op0=ALU.is_le, op1=ALU.mult)
            link(last)
            link(nc.vector.tensor_reduce(cols[:, :], ind[:, :, :], AX.X, ALU.add))
            nc.vector.scalar_tensor_tensor(out=cols[:, 0:2], in0=block_no, scalar=float(P), in1=cols[:, 0:2],
                                           op0=ALU.mult, op1=ALU.add).then_inc(cols_ok, 1)
            link(nc.vector.scalar_tensor_tensor(out=start[:, :], in0=start[:, :], scalar=float(P), in1=first_slot,
                                                op0=ALU.mult, op1=ALU.add))
            nc.vector.memset(low[0][:, 0:EXP], 0.0)
            link(nc.vector.scalar_tensor_tensor(out=low[0][:, EXP:CELLS], in0=nblk[:, 0:CELLS - EXP], scalar=0.0,
                                                in1=cnt[:, 0:CELLS - EXP], op0=ALU.is_gt, op1=ALU.mult))
            least = running(low[0], (low[1], low[0]), EXP, ALU.min)
            dve.wait_ge(colsT_done, 1)
            nc.vector.tensor_copy(tabs[0:1, :], pm[0:1, 0:2 * P])
            link(nc.vector.tensor_tensor(digits[0:1, :, :].rearrange("p i u -> p (i u)"), pm[0:1, 2 * P:2 * P + NB],
                                         powers, ALU.mult))
            link(nc.vector.tensor_reduce(summed[0:1, :], digits[0:1, :, :], AX.X, ALU.add))
            nc.vector.tensor_copy(packed[0:1, :], summed[0:1, :]).then_inc(tabs_ok, 1)
            limits_v, shifts_v = (a[:, :, :].rearrange("p g (e n) -> p (g e) n", n=2) for a in (limits, shifts))
            nc.vector.tensor_copy(limits_v[:, :, 0], first_slot)
            nc.vector.tensor_copy(limits_v[:, :, 1], start[:, :])
            nc.vector.scalar_tensor_tensor(out=shifts_v[:, :, 0], in0=least[:, :], scalar=float(P), in1=first_slot,
                                           op0=ALU.mult, op1=ALU.add)
            link(nc.vector.tensor_copy(shifts_v[:, :, 1], off[:, 0:CELLS]))
            wide = [P, SEQS, 2 * TPS, 2 * EXP]
            nc.vector.tensor_tensor(past[:, :, :, :], slot_all[:, :, :].unsqueeze(3).to_broadcast(wide),
                                    limits[:, :, :].unsqueeze(2).to_broadcast(wide), ALU.is_ge)
            nc.vector.tensor_copy(jumps[:, :, 0], shifts[:, :, 0])
            nc.vector.tensor_tensor(jumps[:, :, 1:], shifts[:, :, 1:], shifts[:, :, 0:2 * EXP - 1], ALU.subtract)\
              .then_inc(limits_ok, 1)

            def slot(at):
                b = at(B_GU)
                if b.live(NB):
                    dve.wait_ge(sil_ok, b.n + 1)
                    wait(dve, ht_done, b.n - 3)
                    nc.vector.tensor_tensor(h[:, b.mod(4), :], sil[:, b.mod(2), :], chb[:, b.mod(2), FF:2 * FF],
                                            ALU.mult).then_inc(h_ok, 1)
                b = at(B_DN)
                if b.live(NB):
                    dve.wait_ge(dn_done, b.n + 1)
                    wait(dve, yb_out[b.mod(4)], b.per(4) * 16)
                    nc.vector.tensor_copy(yb[:, b.mod(4), :], dn_ps[b.mod(2)][:, 0:DIM]).then_inc(yb_ok, 1)

            def combine(m, r):
                k = m * 8 + r
                dve.wait_ge(gath[r], (m + 1) * 32)
                wait(dve, comb_ok, k - 1)
                nc.vector.scalar_tensor_tensor(out=acc[:, r % 2, :], in0=ga[:, r, 0, :], scalar=w12[:, k, 0:1],
                                               in1=xa[:, k, :], op0=ALU.mult, op1=ALU.add).then_inc(acc_ok, 1)
                dve.wait_ge(acc_ok, k + 1)
                wait(dve, stored[r % 4 // 2], (m * 2 + r // 4) * 16)
                nc.vector.scalar_tensor_tensor(out=oo[:, r % 4, :], in0=ga[:, r, 1, :], scalar=w12[:, k, 1:2],
                                               in1=acc[:, r % 2, :], op0=ALU.mult, op1=ALU.add).then_inc(comb_ok, 1)

            def turn(i, m=None, half=0):
                for u in range(U):
                    slot(lambda lag, u=u: At(i, u - lag))
                    if m is not None and u % 2:
                        combine(m, half * TPS + u // 2)

            turn(0)
            turn(1)
            with dve.Fori(2, C_FIRST) as i:
                turn(i)
            turn(C_FIRST, 0, 0)
            turn(C_FIRST + 1, 0, 1)
            in_b = (NB // U - C_FIRST) // 2
            with dve.Fori(1, in_b) as m:
                for half in range(2):
                    turn(m * 2 + C_FIRST + half, m, half)
            turn(NB // U - 1, in_b, 0)
            for s in range(NB, NB + B_STORE):
                slot(lambda lag, s=s: At(s // U, s % U - lag))
            for r in range(TPS, 2 * TPS):
                combine(in_b, r)
            with dve.Fori(in_b + 1, NT // 8) as m:
                for r in range(2 * TPS):
                    combine(m, r)

        @block.gpsimd
        def _(pool):
            def step(at):
                t = at(L_KBD)
                if t.live(NT):
                    pool.wait_ge(kprev_ok, t.n + 1)
                    wait(pool, st_done, 2 * t.n - 6)
                    for par in range(2):
                        last = nc.gpsimd.tensor_tensor(
                            kbd[:, t.mod(4), par, :, :, :],
                            qk[:, t.mod(4), QF:QF + 2 * KF].rearrange("p (h k) -> p h k", h=2).unsqueeze(2)
                            .to_broadcast([P, 2, KV, WIN]),
                            kvmask[:, par, :, :].unsqueeze(1).to_broadcast([P, 2, KV, WIN]), ALU.mult)
                    last.then_inc(kbd_ok, 1)
                t = at(L_RMS)
                if t.live(NT):
                    r = t.mod(4)
                    pool.wait_ge(t12_ok, t.n + 1)
                    nc.gpsimd.tensor_tensor(t3[:, r, :], t1[:, r, :], t2[:, r, :], ALU.add).then_inc(t3_ok, 1)
                    pool.wait_ge(t3_ok, t.n + 1)
                    pool.wait_ge(rms_ok, t.n + 1)
                    wait(pool, tr_ok, t.n - 3)
                    nc.gpsimd.tensor_tensor(t4[:, r, :].rearrange("p (h d) -> p h d", d=HD),
                                            t3[:, r, :].rearrange("p (h d) -> p h d", d=HD),
                                            rr[:, r, :].unsqueeze(2).to_broadcast([P, RF // HD, HD]), ALU.mult)\
                      .then_inc(t4_ok, 1)
                t = at(L_SCAT)
                if t.live(NT):
                    par = t.mod(8) // 4
                    pool.wait_ge(slot_ok, t.per(4) + 1)
                    apart(pool, passed)
                    for k in range(2):
                        nc.gpsimd.indirect_dma_start(
                            xs_dram, bass.IndirectOffsetOnAxis(ap=slot_r[:, par, k, t.mod(4):t.mod(4) + 1], axis=0),
                            xn2[:, t.mod(8), :], None).then_inc(scat[par], 16)

            pool.wait_ge(c_mem, 1)
            pool.wait_ge(c_attn, 20 * 16)
            steps(pool, NT + L_SCAT + 1, PRO, NT, step)

            pool.wait_ge(limits_ok, 1)
            wide = [P, SEQS, 2 * TPS, 2 * EXP]
            link = run(pool, row_chain, 0, 0)
            link(nc.gpsimd.tensor_tensor(past[:, :, :, :], past[:, :, :, :],
                                         jumps[:, :, :].unsqueeze(2).to_broadcast(wide), ALU.mult))
            half = EXP
            while half:
                link(nc.gpsimd.tensor_tensor(past[:, :, :, 0:half], past[:, :, :, 0:half],
                                             past[:, :, :, half:2 * half], ALU.add))
                half //= 2
            link(nc.gpsimd.tensor_tensor(slot_all[:, :, :], slot_all[:, :, :], past[:, :, :, 0], ALU.subtract))
            link(nc.gpsimd.tensor_copy(row_all[:, :, :].rearrange("p (q v) k -> p q (v k)", q=SEQS),
                                       slot_all[:, :, :]))
            for q in range(SEQS):
                blocks = 2 * TPS * (q + 1) + SLACK + 1
                for n in range(4):
                    pool.wait_ge(yb_out[n], blocks // 4 * 16)
                wait(pool, comb_ok, (q - 1) * TPS)
                for v in range(TPS):
                    for j in range(2):
                        nc.gpsimd.indirect_dma_start(
                            ga[:, q % 2 * TPS + v, j, :], None, ys_dram[0:blocks * P, :],
                            bass.IndirectOffsetOnAxis(ap=row_all[:, q * TPS + v, j:j + 1], axis=0))\
                          .then_inc(gath[q % 2 * TPS + v], 16)

    return nc


def _layouts(a):
    heads = [g * J + j for j in range(J) for g in range(KV)]
    qrow = np.array([h * HD + d for h in heads for d in range(HD)])
    swap = np.array([(d + HD // 2) % HD for d in range(HD)])
    qswap = np.array([h * HD + d for h in heads for d in swap])
    kswap = np.array([g * HD + d for g in range(KV) for d in swap])
    partner = np.array([(h ^ 1) * HD + d for h in heads for d in range(HD)])
    wq, wk, wv, wo = (a["L0_attn_" + n] for n in ("Wq", "Wk", "Wv", "Wo"))
    mix = a["L0_attn_pair_mix"]
    hq = np.repeat(np.array(heads), HD)
    return {
        "x": a["L0_attn_x"].reshape(TOK, DIM),
        "w_proj": np.concatenate([wq[qrow], wk, wq[qswap], wk[kswap], wv]).T,
        "gain": np.broadcast_to(a["L0_attn_q_gain"][hq], (P, QF)),
        "wo_self": wo.T[qrow], "wo_pair": wo.T[partner],
        "mix_self": mix[hq // 2, hq % 2, hq % 2][:, None],
        "mix_pair": mix[hq // 2, 1 - hq % 2, hq % 2][:, None],
        "w_router": a["L0_ffn_router_w"].T,
        "w_gu": np.concatenate([a["L0_ffn_w_gate"], a["L0_ffn_w_up"]], axis=1).transpose(2, 0, 1),
        "w_dn": a["L0_ffn_w_down"].reshape(EXP, DIM, 2, P).transpose(3, 0, 2, 1),
    }


def _constants():
    bfloat16 = mybir.dt.np(BF16)
    f = np.float32
    inv = (1.0 / f(10000.0) ** (np.arange(0, HD, 2, dtype=f) / f(HD))).astype(f)
    ang = np.outer(np.arange(SEQ, dtype=f), inv).astype(f)
    cos = np.concatenate([np.cos(ang), np.cos(ang)], 1)
    sin = np.concatenate([np.sin(ang), -np.sin(ang)], 1)
    rope = np.stack([np.concatenate([np.tile(m, (1, HEADS)), np.tile(m, (1, KV)) * HD ** 0.5], 1)
                     for m in (cos, sin)], 1).astype(f)
    own = np.arange(KF) // HD
    kv = (own[:, None] == np.arange(KV)[None, :]).astype(f)
    parity = np.arange(P)[:, None] // WIN % 2 == np.arange(2)[None, :]
    spread = parity[:, :, None] * np.tile(kv, (CH, 1))[:, None, :]
    q, k = np.arange(WIN)[:, None], np.arange(WIN)[None, :]
    cur, old = np.where(k <= q, 0, NEG), np.where(k > q, 0, NEG)
    smq, smk = np.zeros((P, P)), np.zeros((P, 2 * P))
    smq[:WIN] = np.tile(np.eye(WIN), (1, J))
    smk[:WIN] = np.concatenate([np.tile(cur, (1, KV)), np.tile(old, (1, KV))], 1)
    stsel = np.zeros((P, CH, KV, WIN))
    for c in range(CH):
        for g in range(KV):
            stsel[c * KV + g, c, g] = stsel[CH * KV + c * KV + g, c, g] = 1
    stsel[2 * CH * KV:2 * CH * KV + WIN] = np.tile(np.eye(WIN)[:, None, None, :], (1, CH, KV, 1))
    stmask = np.zeros((P - 2 * CH * KV, 2, P))
    stmask[:WIN] = np.stack([np.tile(cur.T, (1, J)), np.tile(old.T, (1, J))], 1)
    cell_e = np.tile(np.arange(EXP), SEQS)
    step_e = np.append(cell_e[1:] - cell_e[:-1], 0)
    cells = np.concatenate([np.broadcast_to(cell_e * CAP, (P, CELLS)), np.broadcast_to(step_e, (P, CELLS)),
                            np.arange(P)[:, None], P + np.arange(P)[:, None],
                            np.broadcast_to(EXP - np.arange(EXP), (P, EXP)),
                            np.broadcast_to(float(EXP) ** (np.arange(NB) % U), (P, NB))], 1)
    return {
        "rope": rope.reshape(TPS, P, 2, RF).transpose(1, 0, 2, 3),
        "ident_in": np.eye(P, dtype=f), "ident16_in": np.eye(P).astype(bfloat16),
        "kvmask_in": np.broadcast_to(spread[:, :, :, None], (P, 2, KV, WIN)).astype(f),
        "oneblk_in": np.repeat(np.repeat(np.eye(KV), WIN, 0), HD, 1).astype(f),
        "smq_in": smq.astype(bfloat16), "smk_in": smk.astype(bfloat16),
        "stsel_in": stsel.reshape(P, CH, P).astype(bfloat16),
        "stmask_in": stmask.astype(bfloat16),
        "tri_in": np.stack([np.triu(np.ones((P, P)), 1), np.ones((P, P))], 1).astype(bfloat16),
        "region_in": np.broadcast_to(np.arange(EXP) * CAP, (P, EXP)).astype(f),
        "cells_in": cells.astype(f),
    }


def kernel(**inputs):
    import concourse.bacc as bacc
    from concourse.bass_utils import run_bass_kernel_spmd

    nc = bacc.Bacc("TRN2", target_bir_lowering=False, num_devices=1)
    given = _layouts({k: np.asarray(v) for k, v in inputs.items()})
    given.update(_constants())
    arrays, args = {}, {}
    for name, a in given.items():
        a = np.ascontiguousarray(a)
        arrays[name] = a
        args[name] = nc.dram_tensor(name, a.shape, mybir.dt.from_np(a.dtype), kind="ExternalInput").ap()
    out = nc.dram_tensor("out", (TOK, DIM), F32, kind="ExternalOutput").ap()
    kernel_body(nc, out=out, **args)
    r = run_bass_kernel_spmd(nc, [arrays], core_ids=[0])
    return r.results[0]["out"].reshape(SEQS, SEQ, DIM)
```
